# Optimizing a Trainium2 kernel written in Bass

```python
import numpy as np
import jax
import jax.numpy as jnp

def _softmax(x, axis=-1):
    return jax.nn.softmax(x, axis=axis)

def _gelu(x):
    return jax.nn.gelu(x, approximate=True)

def _silu(x):
    return jax.nn.silu(x)

def _sigmoid(x):
    return jax.nn.sigmoid(x)

def _layernorm(x, axis=-1, eps=1e-05):
    m = jnp.mean(x, axis=axis, keepdims=True)
    v = jnp.var(x, axis=axis, keepdims=True)
    return (x - m) / jnp.sqrt(v + eps)

def _scatter_add(tgt, idx, src, axis=0):
    return tgt.at[idx].add(src)

def _segment_sum(src, seg, n):
    return jax.ops.segment_sum(src, seg, n)
kernel_name = 'mk_flamingo_gated_d1_seqx_r8_84c938'

def setup_inputs(seed: int=0):
    np.random.seed(seed)
    _w = jnp.asarray

    def _rec_inputs():
        import jax
        import jax.numpy as jnp
        _rk = jax.random.key(seed)
        x = -0.0002928 + 1 * jax.random.normal(jax.random.fold_in(_rk, 1), (32, 128, 128), jnp.float32)
        _lenS = 128 - jax.random.randint(jax.random.fold_in(_rk, 7), (32,), 0, max(1, 128 // 4) + 1, jnp.int32)
        _lenS2 = 128 - jax.random.randint(jax.random.fold_in(_rk, 8), (32,), 0, max(1, 128 // 4) + 1, jnp.int32)
        _ctx_1024P = jax.random.normal(jax.random.fold_in(_rk, 11), (32, 16, 128), jnp.float32)
        _ctx_1024c = jax.random.dirichlet(jax.random.fold_in(_rk, 511), 0.3 * jnp.ones((16,), jnp.float32), (32, 128))
        _ctx_1024t = jnp.einsum('bsk,bkd->bsd', _ctx_1024c, _ctx_1024P)
        _ctx_1024t = _ctx_1024t * jax.lax.rsqrt(jnp.mean(jnp.square(_ctx_1024t)) + 1e-12) * 0.953939
        ctx_1024 = -1.39393e-06 + 0.999914 * (_ctx_1024t + 0.3 * jax.random.normal(jax.random.fold_in(_rk, 611), (32, 128, 128), jnp.float32))
        _g = jax.random.normal(jax.random.fold_in(_rk, 9001), (2, 1), jnp.float32)
        _g = jnp.sign(_g) * jnp.maximum(jnp.abs(_g), 1.0) + (_g == 0) * 1.0
        g_xattn = _g[0]
        g_ffn = _g[1]
        return (x, ctx_1024, g_xattn, g_ffn)
    x, ctx_1024, g_xattn, g_ffn = _rec_inputs()

    def _L0_xattn_setup():
        import jax, jax.numpy as jnp
        import numpy as np
        DIM = 128
        HEADS = 16
        HEAD_DIM = DIM // HEADS
        SCALE = HEAD_DIM ** (-0.5)
        B, N, S = (2, 256, 256)

        def _slice_head(x, W_qkv, b_qkv, idx):
            b, l, _ = x.shape
            qkv = (x @ W_qkv + b_qkv).reshape(b, l, 3, HEADS, HEAD_DIM)
            return jnp.transpose(qkv[:, :, idx], (0, 2, 1, 3))
        key = jax.random.key(seed)
        ks = jax.random.split(key, 5)
        return {'query': jax.random.normal(ks[0], (B, N, DIM), dtype=jnp.float32), 'key': jax.random.normal(ks[1], (B, S, DIM), dtype=jnp.float32), 'value': jax.random.normal(ks[2], (B, S, DIM), dtype=jnp.float32), 'W_qkv': jax.random.normal(ks[3], (DIM, 3 * DIM), dtype=jnp.float32) * DIM ** (-0.5), 'b_qkv': jnp.zeros((3 * DIM,), dtype=jnp.float32), 'W_out': jax.random.normal(ks[4], (DIM, DIM), dtype=jnp.float32) * DIM ** (-0.5), 'b_out': jnp.zeros((DIM,), dtype=jnp.float32)}
    _L0_xattn_all = _L0_xattn_setup()
    _L0_xattn_in = {k: v for k, v in _L0_xattn_all.items() if k in ('W_qkv', 'b_qkv', 'W_out', 'b_out')}
    del _L0_xattn_all

    def _L0_ffn_setup():
        import jax, jax.numpy as jnp
        import numpy as np

        def _moe_forward(x, Wg, W1, b1, W2, b2):
            B, S, H = x.shape
            E = Wg.shape[1]
            tokens = x.reshape(-1, H)
            T = tokens.shape[0]
            C = -(-T // E)
            logits = tokens @ Wg
            gates = jax.nn.softmax(logits, axis=-1)
            idx = jnp.argmax(gates, axis=1)
            mask1 = jax.nn.one_hot(idx, E, dtype=gates.dtype)
            locations1 = jnp.cumsum(mask1, axis=0) - 1.0
            mask1 = mask1 * (locations1 < C).astype(gates.dtype)
            loc_s = jnp.sum(locations1 * mask1, axis=1).astype(jnp.int32)
            gates1 = jnp.sum(gates * mask1, axis=1)
            loc_oh = jax.nn.one_hot(loc_s, C, dtype=gates.dtype)
            dispatch = mask1[:, :, None] * loc_oh[:, None, :]
            combine = gates1[:, None, None] * dispatch
            expert_in = jnp.einsum('tec,th->ech', dispatch, tokens)
            hidden = jax.nn.relu(jnp.einsum('ech,ehf->ecf', expert_in, W1) + b1[:, None, :])
            expert_out = jnp.einsum('ecf,efh->ech', hidden, W2) + b2[:, None, :]
            out = jnp.einsum('tec,ech->th', combine, expert_out)
            return out.reshape(B, S, H)
        key = jax.random.key(seed)
        ks = jax.random.split(key, 6)
        B, S, H, F, E = (4, 256, 128, 512, 8)
        x = jax.random.normal(ks[0], (B, S, H), dtype=jnp.float32)
        Wg = jax.random.normal(ks[1], (H, E), dtype=jnp.float32) * (1.0 / np.sqrt(H))
        W1 = jax.random.normal(ks[2], (E, H, F), dtype=jnp.float32) * (1.0 / np.sqrt(H))
        b1 = jnp.zeros((E, F), dtype=jnp.float32)
        W2 = jax.random.normal(ks[3], (E, F, H), dtype=jnp.float32) * (1.0 / np.sqrt(F))
        b2 = jnp.zeros((E, H), dtype=jnp.float32)
        return {'x': x, 'Wg': Wg, 'W1': W1, 'b1': b1, 'W2': W2, 'b2': b2}
    _L0_ffn_all = _L0_ffn_setup()
    _L0_ffn_in = {k: v for k, v in _L0_ffn_all.items() if k in ('Wg', 'W1', 'b1', 'W2', 'b2')}
    del _L0_ffn_all
    return {'x': x, 'ctx_1024': ctx_1024, 'g_xattn': g_xattn, 'g_ffn': g_ffn, 'L0_xattn_W_qkv': _L0_xattn_in['W_qkv'], 'L0_xattn_b_qkv': _L0_xattn_in['b_qkv'], 'L0_xattn_W_out': _L0_xattn_in['W_out'], 'L0_xattn_b_out': _L0_xattn_in['b_out'], 'L0_ffn_Wg': _L0_ffn_in['Wg'], 'L0_ffn_W1': _L0_ffn_in['W1'], 'L0_ffn_b1': _L0_ffn_in['b1'], 'L0_ffn_W2': _L0_ffn_in['W2'], 'L0_ffn_b2': _L0_ffn_in['b2']}

def reference(x, ctx_1024, g_xattn, g_ffn, L0_xattn_W_qkv, L0_xattn_b_qkv, L0_xattn_W_out, L0_xattn_b_out, L0_ffn_Wg, L0_ffn_W1, L0_ffn_b1, L0_ffn_W2, L0_ffn_b2):
    import jax
    import jax.numpy as jnp

    def _L0_xattn_ref(query, key, value, W_qkv, b_qkv, W_out, b_out):
        import jax, jax.numpy as jnp
        import numpy as np
        DIM = 128
        HEADS = 16
        HEAD_DIM = DIM // HEADS
        SCALE = HEAD_DIM ** (-0.5)
        B, N, S = (2, 256, 256)

        def _slice_head(x, W_qkv, b_qkv, idx):
            b, l, _ = x.shape
            qkv = (x @ W_qkv + b_qkv).reshape(b, l, 3, HEADS, HEAD_DIM)
            return jnp.transpose(qkv[:, :, idx], (0, 2, 1, 3))
        q = _slice_head(query, W_qkv, b_qkv, 0)
        k = _slice_head(key, W_qkv, b_qkv, 1)
        v = _slice_head(value, W_qkv, b_qkv, 2)
        attn = jnp.einsum('bhnd,bhsd->bhns', q, k) * SCALE
        attn = jax.nn.softmax(attn, axis=-1)
        out = jnp.einsum('bhns,bhsd->bhnd', attn, v)
        out = jnp.transpose(out, (0, 2, 1, 3)).reshape(query.shape[0], query.shape[1], DIM)
        return out @ W_out + b_out

    def _L0_ffn_ref(x, Wg, W1, b1, W2, b2):
        import jax, jax.numpy as jnp
        import numpy as np

        def _moe_forward(x, Wg, W1, b1, W2, b2):
            B, S, H = x.shape
            E = Wg.shape[1]
            tokens = x.reshape(-1, H)
            T = tokens.shape[0]
            C = -(-T // E)
            logits = tokens @ Wg
            gates = jax.nn.softmax(logits, axis=-1)
            idx = jnp.argmax(gates, axis=1)
            mask1 = jax.nn.one_hot(idx, E, dtype=gates.dtype)
            locations1 = jnp.cumsum(mask1, axis=0) - 1.0
            mask1 = mask1 * (locations1 < C).astype(gates.dtype)
            loc_s = jnp.sum(locations1 * mask1, axis=1).astype(jnp.int32)
            gates1 = jnp.sum(gates * mask1, axis=1)
            loc_oh = jax.nn.one_hot(loc_s, C, dtype=gates.dtype)
            dispatch = mask1[:, :, None] * loc_oh[:, None, :]
            combine = gates1[:, None, None] * dispatch
            expert_in = jnp.einsum('tec,th->ech', dispatch, tokens)
            hidden = jax.nn.relu(jnp.einsum('ech,ehf->ecf', expert_in, W1) + b1[:, None, :])
            expert_out = jnp.einsum('ecf,efh->ech', hidden, W2) + b2[:, None, :]
            out = jnp.einsum('tec,ech->th', combine, expert_out)
            return out.reshape(B, S, H)
        return _moe_forward(x, Wg, W1, b1, W2, b2)
    x = x + jnp.tanh(g_xattn[0]) * _L0_xattn_ref(_layernorm(x, axis=-1), ctx_1024, ctx_1024, L0_xattn_W_qkv, L0_xattn_b_qkv, L0_xattn_W_out, L0_xattn_b_out)
    x = x + jnp.tanh(g_ffn[0]) * _L0_ffn_ref(_layernorm(x, axis=-1), L0_ffn_Wg, L0_ffn_W1, L0_ffn_b1, L0_ffn_W2, L0_ffn_b2)
    return x

_drawn_inputs = setup_inputs


def setup_inputs(seed=0):
    import zlib

    import numpy as np

    out = dict(_drawn_inputs(seed))
    spreads = {'L0_xattn_b_qkv': (0.0, 0.1),
     'L0_xattn_b_out': (0.0, 0.1),
     'L0_ffn_b1': (0.0, 0.36),
     'L0_ffn_b2': (0.0, 0.1)}
    factors = {}
    for name, (base, spread) in spreads.items():
        noise = np.random.default_rng([zlib.crc32(name.encode()), seed]).standard_normal(out[name].shape)
        drawn = base * np.exp(spread * noise) if base else spread * noise
        out[name] = jnp.asarray(drawn.astype(out[name].dtype))
    for name, factor in factors.items():
        out[name] = (out[name] * factor).astype(out[name].dtype)
    return out
```

```python
from contextlib import ExitStack

import concourse.bass as bass
from concourse import mybir

F32 = mybir.dt.float32
BF16 = mybir.dt.bfloat16
U32 = mybir.dt.uint32
ALU = mybir.AluOpType
ACT = mybir.ActivationFunctionType
AX = mybir.AxisListType

P = 128
GB = 4
BODY = 8
EPS = 1e-5
Q_PARTS = (0, 0, 0, 1, 1, 2)
K_PARTS = (0, 1, 2, 0, 1, 0)
REC = 2 * P + 2


def flamingo_kernel(nc, x, ctx_in, g_xattn, g_ffn, w_qkv, b_qkv, w_out, b_out, wg, w1, b1, w2, b2, consts, out):
    B, L, D = x.shape
    E, _, F = w1.shape
    T = B * L
    CAP = -(-T // E)
    HEADS = 16
    HD = D // HEADS
    HV = 32
    SCALE = float(HD) ** -0.5
    NG = B // GB
    GT = GB * L
    SLOTS = len(Q_PARTS)
    KR = SLOTS * HD
    KM = KR + 2
    FC = F // P
    ET = CAP // P
    NONE = 2 * T
    LOOP0, LOOP1 = BODY, B - BODY
    FIRST, LAST = -7, 4 * (NG - 1) + 11
    assert L == P and D == P and CAP == 4 * P and F == 4 * P and E == 8

    with ExitStack() as ctx:
        def sb(name, shape, dt=F32):
            return ctx.enter_context(nc.sbuf_tensor(name, shape, dt))

        def ps(name):
            return ctx.enter_context(nc.psum_tensor(name, [P, 2, 512], F32))

        def sem(name):
            return ctx.enter_context(nc.semaphore(name))

        def sem2(name):
            return [sem(name + "0"), sem(name + "1")]

        rec_dram = nc.dram_tensor("rec_dram", (T, REC), F32).ap()

        S = ps("S")
        TS = ps("TS")
        O = ps("O")
        X = ps("X")

        cst = sb("cst", [P, 2 * P + GB * E + B])
        ident = cst[:, 0:P]
        iota = cst[:, 2 * P:2 * P + GB * E].rearrange("p (k e) -> p k e", e=E)
        token_code = cst[:, 2 * P + GB * E:]
        ident_b = sb("ident_b", [P, P], BF16)
        before_b = sb("before_b", [P, P], BF16)
        ones_b = sb("ones_b", [P, P], BF16)
        wqkv = sb("wqkv", [P, 3 * D])
        wq_dh = sb("wq_dh", [P, D])
        wk_dh = sb("wk_dh", [P, D])
        bqk = sb("bqk", [P, 2])
        bq_s = sb("bq_s", [P, 1])
        bv = sb("bv", [P, D])
        wout = sb("wout", [P, D])
        wout_g = sb("wout_g", [P, D])
        bout = sb("bout", [P, D])
        bout_g = sb("bout_g", [P, D])
        wg_sb = sb("wg_sb", [P, E])
        gains = sb("gains", [P, 2])
        tg = sb("tg", [P, 2])
        pool_c = sb("pool_c", [P, 2, GB])
        zeros = sb("zeros", [P, T // P // 8 * REC])
        fence_v = sb("fence_v", [P, 4])
        fence_p = sb("fence_p", [P, 1])

        x_sb = sb("x_sb", [P, B, D])
        c_sb = [sb(f"c_sb{i}", [P, GB, D]) for i in range(2)]
        cT = [sb(f"cT{i}", [P, GT]) for i in range(2)]
        xn = sb("xn", [P, GB, D])
        xnT = sb("xnT", [P, GT])
        st1 = sb("st1", [P, GB, 6])
        mv1 = sb("mv1", [P, GB, 2])
        rs1 = sb("rs1", [P, 2, GB])
        full = [sb(f"full_{s}", [P, GT]) for s in "qk"]
        rest = [sb(f"rest_{s}", [P, GT]) for s in "qk"]
        parts = [[sb(f"parts_{s}{i}", [P, 3, GT], BF16) for i in range(2)] for s in "qk"]
        qp = [sb(f"qp{i}", [P, HEADS, GT], BF16) for i in range(2)]
        kp = [sb(f"kp{i}", [P, HEADS, GT], BF16) for i in range(2)]
        vals = [sb(f"vals{i}", [P, GB, HEADS, HV]) for i in range(2)]
        ones_row = sb("ones_row", [2 * HEADS, GT], BF16)
        oraw = [sb(f"oraw{i}", [P, 4 * L]) for i in range(2)]
        negm = [sb(f"negm{i}", [P, HEADS]) for i in range(2)]
        mpart = [sb(f"mpart{i}", [P, 2, HEADS], BF16) for i in range(2)]
        mrow = [sb(f"mrow{i}", [2 * HEADS, P], BF16) for i in range(2)]
        prob = [sb(f"prob{i}", [P, HEADS * L]) for i in range(2)]
        rl = sb("rl", [P, HEADS])
        on = [sb(f"on{i}", [P, D]) for i in range(2)]
        onT = [sb(f"onT{i}", [P, L]) for i in range(2)]
        st2 = sb("st2", [P, GB, 6])
        mv2 = sb("mv2", [P, GB, 2])
        rs2 = sb("rs2", [P, 2, GB])
        rec = [sb(f"rec{i}", [P, GB, REC]) for i in range(2)]
        xn2T = sb("xn2T", [P, GT])
        lgs = sb("lgs", [P, GB, E])
        lmax = sb("lmax", [P, GB])
        ldif = sb("ldif", [P, GB, E])
        lexp = sb("lexp", [P, GB, E])
        lsum = sb("lsum", [P, GB])
        cand = sb("cand", [P, GB, E])
        choice = sb("choice", [P, GB])
        mask = sb("mask", [P, GB, E], BF16)
        seen = sb("seen", [P, E], BF16)
        seen_g = sb("seen_g", [P, E])
        at_e = sb("at_e", [P, GB, E])
        loc = sb("loc", [P, GB])
        over = sb("over", [P, GB])
        base = sb("base", [P, GB])
        slot = [sb(f"slot{i}", [P, GB], U32) for i in range(2)]
        w1s = [sb(f"w1s{i}", [P, F]) for i in range(2)]
        w2s = [sb(f"w2s{i}", [P, FC, D]) for i in range(2)]
        b1s = [sb(f"b1s{i}", [P, FC]) for i in range(2)]
        b2s = [sb(f"b2s{i}", [P, D]) for i in range(2)]
        xe = [sb(f"xe{i}", [P, ET, REC]) for i in range(2)]
        xeT = [sb(f"xeT{i}", [P, CAP]) for i in range(2)]
        hid = [qp[i][:, 0:8, :].rearrange("p h n -> p (h n)").bitcast(F32).rearrange("p (f n) -> p f n", f=FC)
               for i in range(2)]
        yb = sb("yb", [P, CAP])
        gate2 = [sb(f"gate2_{i}", [P, ET]) for i in range(2)]
        tok = [sb(f"tok{i}", [P, ET], U32) for i in range(2)]
        fin = [sb(f"fin{i}", [P, ET, D]) for i in range(2)]

        s_cst, s_wqkv, s_bias, s_late = sem("s_cst"), sem("s_wqkv"), sem("s_bias"), sem("s_late")
        s_zero, s_vset, s_tanh, s_pset = sem("s_zero"), sem("s_vset"), sem("s_tanh"), sem("s_pset")
        x_in = [sem(f"x_in{i}") for i in range(3)]
        c_in, q_in, k_in, m_in = sem2("c_in"), sem2("q_in"), sem2("k_in"), sem2("m_in")
        x1_out, sent = sem("x1_out"), sem2("sent")
        p_cT, p_xT, p_q, p_k, p_v = sem("p_cT"), sem("p_xT"), sem("p_q"), sem("p_k"), sem("p_v")
        g_zero = sem("g_zero")
        v_ones, g_vals = sem("v_ones"), sem("g_vals")
        p_back, a_O, s_ones = sem("p_back"), sem("a_O"), sem("s_ones")
        p_S, p_m, p_T, p_O, p_oT, p_at = sem("p_S"), sem("p_m"), sem("p_T"), sem("p_O"), sem("p_oT"), sem("p_at")
        p_nT, p_lg, p_pos = sem("p_nT"), sem("p_lg"), sem("p_pos")
        a_cT, a_xT, a_q, a_k, a_m = sem("a_cT"), sem("a_xT"), sem("a_q"), sem("a_k"), sem("a_m")
        a_exp, a_oT, a_nT, a_lexp, a_rec = sem("a_exp"), sem("a_oT"), sem("a_nT"), sem("a_lexp"), sem("a_rec")
        v_st1, v_mv1, v_xn, v_v, v_red, v_m1, v_m = (sem("v_st1"), sem("v_mv1"), sem("v_xn"), sem("v_v"), sem("v_red"),
                                                     sem("v_m1"), sem("v_m"))
        v_rl, v_on, v_x1, v_st2, v_mv2, v_xn2 = sem("v_rl"), sem("v_on"), sem("v_x1"), sem("v_st2"), sem("v_mv2"), sem("v_xn2")
        v_lg, v_ldif, v_route, v_mask, v_pos, v_place, v_slot = (sem("v_lg"), sem("v_ldif"), sem("v_route"), sem("v_mask"),
                                                                sem("v_pos"), sem("v_place"), sem("v_slot"))
        g_e1, g_rs1, g_e2, g_rs2, g_xb, g_spl, g_q, g_k = (sem("g_e1"), sem("g_rs1"), sem("g_e2"), sem("g_rs2"), sem("g_xb"),
                                                           sem("g_spl"), sem("g_q"), sem("g_k"))
        g_fence = sem("g_fence")
        w_in, e_in, fin_out = sem2("w_in"), sem2("e_in"), sem2("fin_out")
        p_eT, p_H, p_Y = sem("p_eT"), sem("p_H"), sem("p_Y")
        a_eT, a_H, v_H, v_yb, v_gate2, v_tok, v_fin = (sem("a_eT"), sem("a_H"), sem("v_H"), sem("v_yb"), sem("v_gate2"),
                                                       sem("v_tok"), sem("v_fin"))

        x_v = x.rearrange("b p d -> p b d")
        out_v = out.rearrange("b p d -> p b d")
        out_rows = out.rearrange("b p d -> (b p) d")
        ctx_v = ctx_in.rearrange("b p d -> p b d")
        rec_v = rec_dram.rearrange("(e t p) c -> e p t c", t=ET, p=P)

        def per_batch(v, r, per=1):
            return v if r is None else r * (per * BODY) + v

        def per_group(v, r, per=1):
            return v if r is None else r * (per * BODY // GB) + v

        def is_batch(n):
            return 0 <= n < B

        def is_group(g):
            return 0 <= g < NG

        BATCH_TASKS = ("m", "at", "back", "oT")

        def x_tasks(c):
            j, g = c % GB, c // GB
            first = {0: ("v", g), 2: ("cT", g + 2), 3: ("k", g + 2)}.get(j)
            third = {2: ("lg", g - 2), 3: ("pos", g - 2)}.get(j)
            second = {1: ("nT", g - 2), 2: ("xT", g + 2), 3: ("q", g + 2)}.get(j)
            bank0 = [("m", c - 1), ("at", c - 5), second]
            bank1 = [first, ("back", c - 4), third, ("oT", c - 4)]
            ok = lambda t: t is not None and (is_batch(t[1]) if t[0] in BATCH_TASKS else is_group(t[1]))
            return [[t for t in bank0 if ok(t)], [t for t in bank1 if ok(t)]]

        before = {}
        for bank in range(2):
            last = None
            for c in range(FIRST, LAST + 1):
                for t in x_tasks(c)[bank]:
                    before[t] = last
                    last = t
        emptied = {"v": v_v, "cT": a_cT, "k": a_k, "lg": v_lg, "pos": v_pos, "nT": a_nT, "xT": a_xT, "q": a_q,
                   "m": a_m, "at": v_x1, "back": v_on, "oT": a_oT}

        def bank_free(eng, name, idx, r):
            t = before[(name, idx)]
            if t is not None:
                step = per_batch if t[0] in BATCH_TASKS else per_group
                eng.wait_ge(emptied[t[0]], step(t[1] + 1, r))

        def run_steps(step_fn, eng):
            for c in range(FIRST, LOOP0):
                step_fn(c, None)
            with eng.Fori(0, (LOOP1 - LOOP0) // BODY) as r:
                for c in range(LOOP0, LOOP0 + BODY):
                    step_fn(c, r)
            for c in range(LOOP1, LAST + 1):
                step_fn(c, None)

        block = ctx.enter_context(nc.Block())

        @block.sync
        def _(sp):
            sp.dma_start(x_sb[:, 0:GB, :], x_v[:, 0:GB, :]).then_inc(x_in[0], 16)
            sp.dma_start(cst[:], consts).then_inc(s_cst, 16)
            sp.dma_start(wqkv[:], w_qkv).then_inc(s_wqkv, 16)
            for i in range(2):
                sp.dma_start(bqk[:, i:i + 1], b_qkv[i * D:(i + 1) * D].rearrange("(h d o) -> d h o", d=HD, o=1),
                             allow_slow_non_contiguous=True).then_inc(s_bias, 16)
            sp.dma_start(gains[:, 0:1], g_xattn.rearrange("(a n) -> a n", a=1).broadcast_to([P, 1])).then_inc(s_bias, 16)
            sp.dma_start(gains[:, 1:2], g_ffn.rearrange("(a n) -> a n", a=1).broadcast_to([P, 1])).then_inc(s_bias, 16)

            def moved(view, offset):
                return view if offset is None else bass.AP(view.tensor, offset, view.ap)

            def weights(p, e, at):
                a1, a2, a3, a4 = at
                sp.dma_start(w1s[p][:], moved(w1[e], a1)).then_inc(w_in[p], 16)
                sp.dma_start(w2s[p][:], moved(w2[e].rearrange("(f p) n -> p f n", p=P), a2)).then_inc(w_in[p], 16)
                sp.dma_start(b1s[p][:], moved(b1[e].rearrange("(f p) -> p f", p=P), a3),
                             allow_slow_non_contiguous=True).then_inc(w_in[p], 16)
                sp.dma_start(b2s[p][:], moved(b2[e:e + 1].broadcast_to([P, D]), a4)).then_inc(w_in[p], 16)

            scratch = sp.alloc_register("ready")

            def ready(*values):
                for v in values:
                    if not isinstance(v, int):
                        sp.reg_mov(scratch, v)

            def late_loads():
                sp.dma_start(x_sb[:, GB:2 * GB, :], x_v[:, GB:2 * GB, :]).then_inc(x_in[1], 16)
                sp.dma_start(bv[:], b_qkv[2 * D:3 * D].rearrange("(a n) -> a n", a=1).broadcast_to([P, D])).then_inc(s_late, 16)
                sp.dma_start(bout[:], b_out.rearrange("(a n) -> a n", a=1).broadcast_to([P, D])).then_inc(s_late, 16)
                sp.dma_start(wout[:], w_out).then_inc(s_late, 16)
                sp.dma_start(wg_sb[:], wg).then_inc(s_late, 16)

            def step(c, r):
                j, g = c % GB, c // GB
                loads, stores = j == 1 and is_group(g + 2), j == 1 and is_group(g - 2)
                if j == 1:
                    ready(per_batch(c, r), per_group(g + 1, r), per_batch(GB * (g - 2) + GB, r))
                if is_batch(c - 1):
                    sp.wait_ge(a_m, per_batch(c, r))
                if loads and g + 2 >= 2:
                    sp.wait_ge(p_cT, per_group(g + 1, r))
                if stores:
                    sp.wait_ge(v_x1, per_batch(GB * (g - 2) + GB, r))
                if is_batch(c - 1):
                    n, p = c - 1, (c - 1) % 2
                    G = n // GB
                    t0 = (n % GB) * L
                    sp.dma_start(qp[G % 2][KR:KM, :, t0:t0 + L], mrow[p][:]).then_inc(m_in[p], 16)
                if loads:
                    sp.dma_start(c_sb[g % 2][:], ctx_v[:, bass.ds(per_group((g + 2) * GB, r, GB), GB), :]).then_inc(c_in[g % 2], 16)
                if stores:
                    sl = bass.ds(per_group((g - 2) * GB, r, GB), GB)
                    sp.dma_start(out_v[:, sl, :], x_sb[:, sl, :]).then_inc(x1_out, 16)
                if is_group(g + 1) and j in (2, 3):
                    H, p = g + 1, (g + 1) % 2
                    if j == 2:
                        ready(per_batch(4 * (GB * H - 5) + 4, r, 4), per_group(H + 1, r))
                        if H >= 2:
                            sp.wait_ge(p_T, per_batch(4 * (GB * H - 5) + 4, r, 4))
                        sp.wait_ge(g_k, per_group(H + 1, r))
                        sp.wait_ge(a_k, per_group(H + 1, r))
                    pieces = [("k", s) for s in range(SLOTS)] + [("q", s) for s in range(SLOTS)]
                    for side, s in (pieces[:8] if j == 2 else pieces[8:]):
                        if (side, s) == ("q", 0):
                            sp.wait_ge(g_q, per_group(H + 1, r))
                            sp.wait_ge(a_q, per_group(H + 1, r))
                        dst = (kp if side == "k" else qp)[p][s * HD:(s + 1) * HD, :, :]
                        src = parts[side == "k"][p][:, (K_PARTS if side == "k" else Q_PARTS)[s], :]
                        sp.dma_start(dst, src).then_inc((k_in if side == "k" else q_in)[p], 16)
                if c == -7:
                    late_loads()
                if c == 0:
                    sp.dma_start(x_sb[:, 2 * GB:, :], x_v[:, 2 * GB:, :]).then_inc(x_in[2], 16)
                if c == -1:
                    sp.wait_ge(v_ones, 1)
                    for i in range(2):
                        sp.dma_start(kp[i][KR:KM, :, :], ones_row[:]).then_inc(s_ones, 16)
                if c == 2:
                    weights(0, 0, (None,) * 4)
                    weights(1, 1, (None,) * 4)

            run_steps(step, sp)

            def records(e, at):
                sp.dma_start(xe[e % 2][:], moved(rec_v[e], at)).then_inc(e_in[e % 2], 16)

            for p in range(2):
                sp.wait_ge(sent[p], 64 + 16 * GB * (NG // 2))
            records(0, None)
            records(1, None)
            with sp.Fori(0, (E - 2) // 2) as r:
                for e in (2, 3):
                    w_at, rec_at = r * (2 * D * F) + e * D * F, r * (2 * CAP * REC) + e * CAP * REC
                    at = (w_at, w_at, r * (2 * F) + e * F, r * (2 * D) + e * D)
                    through = r * 2 + (e - 1)
                    ready(w_at * 4, at[2] * 4, at[3] * 4, rec_at * 4)
                    sp.wait_ge(v_fin, through)
                    records(e, rec_at)
                    weights(e % 2, 0, at)
            sp.wait_ge(x1_out, 16 * NG)
            for p in range(2):
                sp.wait_ge(fin_out[p], 16 * ET * (E // 2))

        @block.tensor
        def _(pe):
            def group_task(name, idx, r):
                bank_free(pe, name, idx, r)
                if name == "cT":
                    pe.wait_ge(c_in[idx % 2], per_group(16 * (idx // 2) + 16, r, 8))
                    if idx == 0:
                        pe.wait_ge(s_cst, 16)
                    for k in range(GB):
                        mm = nc.tensor.transpose(X[:, 1, k * L:(k + 1) * L], c_sb[idx % 2][:, k, :], ident)
                    mm.then_inc(p_cT, 1)
                elif name == "xT":
                    pe.wait_ge(v_xn, per_group(idx + 1, r))
                    for k in range(GB):
                        mm = nc.tensor.transpose(X[:, 0, k * L:(k + 1) * L], xn[:, k, :], ident)
                    mm.then_inc(p_xT, 1)
                elif name == "k":
                    pe.wait_ge(a_cT, per_group(idx + 1, r))
                    if idx == 0:
                        pe.wait_ge(s_vset, 1)
                    nc.tensor.matmul(X[:, 1, :], wk_dh[:], cT[idx % 2][:], start=True, stop=True).then_inc(p_k, 1)
                elif name == "q":
                    pe.wait_ge(a_xT, per_group(idx + 1, r))
                    nc.tensor.matmul(X[:, 0, :], wq_dh[:], xnT[:], start=True, stop=True).then_inc(p_q, 1)
                elif name == "v":
                    for k in range(GB):
                        mm = nc.tensor.matmul(X[:, 1, k * L:(k + 1) * L], cT[idx % 2][:, k * L:(k + 1) * L],
                                              wqkv[:, 2 * D:3 * D], start=True, stop=True)
                    mm.then_inc(p_v, 1)
                elif name == "nT":
                    pe.wait_ge(v_xn2, per_group(idx + 1, r))
                    for k in range(GB):
                        mm = nc.tensor.transpose(X[:, 0, k * L:(k + 1) * L], rec[idx % 2][:, k, 0:D], ident)
                    mm.then_inc(p_nT, 1)
                elif name == "lg":
                    pe.wait_ge(a_nT, per_group(idx + 1, r))
                    for k in range(GB):
                        mm = nc.tensor.matmul(X[:, 1, k * E:(k + 1) * E], xn2T[:, k * L:(k + 1) * L], wg_sb[:],
                                              start=True, stop=True)
                    mm.then_inc(p_lg, 1)
                elif name == "pos":
                    pe.wait_ge(v_mask, per_group(idx + 1, r))
                    for k in range(GB):
                        o = X[:, 1, k * E:(k + 1) * E]
                        nc.tensor.matmul(o, before_b[:], mask[:, k, :], start=True, stop=False)
                        for k2 in range(k):
                            nc.tensor.matmul(o, ones_b[:], mask[:, k2, :], start=False, stop=False)
                        mm = nc.tensor.matmul(o, ones_b[:], seen[:], start=False, stop=True)
                    mm.then_inc(p_pos, 1)

            def scores(n, q, r):
                G, t0 = n // GB, (n % GB) * L
                if q == 0 and n % GB == 0:
                    pe.wait_ge(q_in[G % 2], per_group(96 * (G // 2) + 96, r, 48))
                    pe.wait_ge(k_in[G % 2], per_group(96 * (G // 2) + 96, r, 48))
                if 4 * n + q >= 2:
                    pe.wait_ge(v_red, per_batch(4 * n + q - 1, r, 4))
                for h in range(4 * q, 4 * q + 4):
                    o = (h % 4) * L
                    mm = nc.tensor.matmul(S[:, q % 2, o:o + L], qp[G % 2][0:KR, h, t0:t0 + L],
                                          kp[G % 2][0:KR, h, t0:t0 + L], start=True, stop=True)
                mm.then_inc(p_S, 1)

            def shifted(n, q, r):
                G, t0 = n // GB, (n % GB) * L
                if q == 0:
                    if n == 0:
                        pe.wait_ge(s_ones, 32)
                    pe.wait_ge(m_in[n % 2], per_batch(16 * (n // 2) + 16, r, 8))
                if 4 * n + q >= 2:
                    pe.wait_ge(a_exp, per_batch(4 * n + q - 1, r, 4))
                for h in range(4 * q, 4 * q + 4):
                    o = (h % 4) * L
                    mm = nc.tensor.matmul(TS[:, q % 2, o:o + L], kp[G % 2][0:KM, h, t0:t0 + L],
                                          qp[G % 2][0:KM, h, t0:t0 + L], start=True, stop=True)
                mm.then_inc(p_T, 1)

            def values(n, q, r):
                G, k = n // GB, n % GB
                pe.wait_ge(a_exp, per_batch(4 * n + q + 1, r, 4))
                if q == 0:
                    if k == 0:
                        pe.wait_ge(v_v, per_group(G + 1, r))
                    if n >= 2:
                        pe.wait_ge(a_O, per_batch(n - 1, r))
                for h in range(4 * q, 4 * q + 4):
                    i = h % 4
                    mm = nc.tensor.matmul(O[i * HV:(i + 1) * HV, n % 2, q * L:(q + 1) * L], vals[G % 2][:, k, h, :],
                                          prob[n % 2][:, h * L:(h + 1) * L], start=True, stop=True)
                if q == 3:
                    mm.then_inc(p_O, 1)

            def step(c, r):
                todo = x_tasks(c)
                groups = [t for bank in todo for t in bank if t[0] not in BATCH_TASKS]
                at_q = {0: [t for t in groups if t[0] in ("v", "cT", "k")], 1: [],
                        2: [t for t in groups if t[0] in ("lg", "pos", "nT", "xT", "q")], 3: []}
                for q in range(4):
                    if is_batch(c):
                        scores(c, q, r)
                    if is_batch(c - 2):
                        shifted(c - 2, q, r)
                    if q == 0 and is_batch(c - 1):
                        bank_free(pe, "m", c - 1, r)
                        pe.wait_ge(v_m, per_batch(c, r))
                        nc.tensor.transpose(X[:, 0, 0:P // 2].bitcast(BF16)[0:2 * HEADS, :],
                                            mpart[(c - 1) % 2][:].rearrange("p j h -> p (j h)"), ident_b[:]).then_inc(p_m, 1)
                    for t in at_q[q]:
                        group_task(t[0], t[1], r)
                    if q == 1 and is_batch(c - 5):
                        bank_free(pe, "at", c - 5, r)
                        pe.wait_ge(a_oT, per_batch(c - 4, r))
                        nc.tensor.matmul(X[:, 0, 0:D], onT[(c - 5) % 2][:], wout_g[:], start=True, stop=True).then_inc(p_at, 1)
                    if q == 1 and is_batch(c - 4):
                        bank_free(pe, "back", c - 4, r)
                        pe.wait_ge(a_O, per_batch(c - 3, r))
                        for i in range(4):
                            mm = nc.tensor.transpose(X[:, 1, i * L:(i + 1) * L], oraw[c % 2][:, i * L:(i + 1) * L], ident)
                        mm.then_inc(p_back, 1)
                    if q == 3 and is_batch(c - 4):
                        bank_free(pe, "oT", c - 4, r)
                        pe.wait_ge(v_on, per_batch(c - 3, r))
                        nc.tensor.transpose(X[:, 1, 0:L], on[c % 2][:], ident).then_inc(p_oT, 1)
                    if is_batch(c - 3):
                        values(c - 3, q, r)

            run_steps(step, pe)

            def two(v, r, per=1):
                return v if r is None else r * (2 * per) + v

            def turn(e, r):
                pe.wait_ge(e_in[e % 2], two(16 * (e // 2) + 16, r, 8))
                if e >= 2:
                    pe.wait_ge(a_eT, two(e - 1, r))
                for t in range(ET):
                    mm = nc.tensor.transpose(S[:, e % 2, t * P:(t + 1) * P], xe[e % 2][:, t, 0:D], ident)
                mm.then_inc(p_eT, 1)

            def hidden(e, r):
                pe.wait_ge(a_eT, two(e + 1, r))
                pe.wait_ge(w_in[e % 2], two(64 * (e // 2) + 64, r, 32))
                for f in range(FC):
                    if e >= 1:
                        pe.wait_ge(a_H if f % 2 == 0 else v_H, two(2 * (e - 1) + f // 2 + 1, r, 2))
                    bank = (TS if f % 2 == 0 else O)[:, f // 2, :]
                    nc.tensor.matmul(bank, w1s[e % 2][:, f * P:(f + 1) * P], xeT[e % 2][:], start=True, stop=True).then_inc(p_H, 1)

            def outputs(e, r):
                pe.wait_ge(a_H, two(2 * e + 2, r, 2))
                pe.wait_ge(v_H, two(2 * e + 2, r, 2))
                if e >= 2:
                    pe.wait_ge(v_yb, two(e - 1, r))
                for t in range(ET):
                    for f in range(FC):
                        mm = nc.tensor.matmul(X[:, e % 2, t * P:(t + 1) * P], hid[e % 2][:, f, t * P:(t + 1) * P],
                                              w2s[e % 2][:, f, :], start=(f == 0), stop=(f == FC - 1))
                mm.then_inc(p_Y, 1)

            turn(0, None)
            hidden(0, None)
            turn(1, None)
            hidden(1, None)
            outputs(0, None)
            turn(2, None)
            hidden(2, None)
            outputs(1, None)
            with pe.Fori(0, (E - 4) // 2) as r:
                for e in (3, 4):
                    turn(e, r)
                    hidden(e, r)
                    outputs(e - 1, r)
            turn(E - 1, None)
            hidden(E - 1, None)
            outputs(E - 2, None)
            outputs(E - 1, None)

        @block.scalar
        def _(act):
            def proj(side, H, r):
                ready, done, bank = ((p_q, a_q, 0), (p_k, a_k, 1))[side]
                act.wait_ge(ready, per_group(H + 1, r))
                if H >= 1:
                    act.wait_ge((g_q, g_k)[side], per_group(H, r))
                if H >= 2:
                    act.wait_ge((q_in, k_in)[side][H % 2], per_group(96 * (H // 2), r, 48))
                bias = bq_s[:, 0:1] if side == 0 else bqk[:, 1:2]
                sc = SCALE if side == 0 else 1.0
                nc.scalar.activation(full[side][:], X[:, bank, :], ACT.Identity, bias=bias, scale=sc)
                nc.scalar.activation(parts[side][H % 2][:, 0, :], X[:, bank, :], ACT.Identity, bias=bias,
                                     scale=sc).then_inc(done, 1)

            def exps(n, q, r):
                act.wait_ge(p_T, per_batch(4 * n + q + 1, r, 4))
                if n >= 2:
                    if q == 0:
                        act.wait_ge(p_O, per_batch(n - 1, r))
                nc.scalar.activation(prob[n % 2][:, q * 512:(q + 1) * 512], TS[:, q % 2, :], ACT.Exp).then_inc(a_exp, 1)

            def step(c, r):
                j, g = c % GB, c // GB
                if is_batch(c - 1):
                    n = c - 1
                    act.wait_ge(p_m, per_batch(n + 1, r))
                    if n >= 2:
                        act.wait_ge(m_in[n % 2], per_batch(16 * (n // 2), r, 8))
                    nc.scalar.activation(mrow[n % 2][:], X[:, 0, 0:P // 2].bitcast(BF16)[0:2 * HEADS, :],
                                         ACT.Copy).then_inc(a_m, 1)
                if is_batch(c - 4):
                    n = c - 4
                    act.wait_ge(p_O, per_batch(n + 1, r))
                    if n >= 2:
                        act.wait_ge(p_back, per_batch(n - 1, r))
                    nc.scalar.activation(oraw[n % 2][:], O[:, n % 2, :], ACT.Copy).then_inc(a_O, 1)
                if is_batch(c - 2):
                    exps(c - 2, 0, r)
                if j == 2 and is_group(g + 2):
                    H = g + 2
                    act.wait_ge(p_cT, per_group(H + 1, r))
                    if H >= 2:
                        act.wait_ge(p_v, per_group(H - 1, r))
                    nc.scalar.activation(cT[H % 2][:], X[:, 1, :], ACT.Copy).then_inc(a_cT, 1)
                if j == 3 and is_group(g + 2):
                    proj(1, g + 2, r)
                if is_batch(c - 2):
                    exps(c - 2, 1, r)
                if is_batch(c - 2):
                    exps(c - 2, 2, r)
                if j == 1 and is_group(g - 2):
                    G = g - 2
                    act.wait_ge(p_nT, per_group(G + 1, r))
                    nc.scalar.activation(xn2T[:], X[:, 0, :], ACT.Copy).then_inc(a_nT, 1)
                if j == 2 and is_group(g + 2):
                    H = g + 2
                    act.wait_ge(p_xT, per_group(H + 1, r))
                    if H >= 1:
                        act.wait_ge(p_q, per_group(H, r))
                    nc.scalar.activation(xnT[:], X[:, 0, :], ACT.Copy).then_inc(a_xT, 1)
                if j == 3 and is_group(g + 2):
                    proj(0, g + 2, r)
                if is_batch(c - 2):
                    exps(c - 2, 3, r)
                if is_batch(c - 4):
                    n = c - 4
                    act.wait_ge(p_oT, per_batch(n + 1, r))
                    if n >= 2:
                        act.wait_ge(p_at, per_batch(n - 1, r))
                    nc.scalar.activation(onT[n % 2][:], X[:, 1, 0:L], ACT.Copy).then_inc(a_oT, 1)
                if j == 1 and is_group(g - 2):
                    G = g - 2
                    act.wait_ge(v_xn2, per_group(G + 1, r))
                    nc.scalar.activation(rec[G % 2][:, :, D:2 * D], x_sb[:, bass.ds(per_group(G * GB, r, GB), GB), :],
                                         ACT.Copy).then_inc(a_rec, 1)
                if j == 2 and is_group(g - 2):
                    G = g - 2
                    act.wait_ge(v_ldif, per_group(G + 1, r))
                    nc.scalar.activation(lexp[:], ldif[:], ACT.Exp).then_inc(a_lexp, 1)

            act.wait_ge(s_bias, 64)
            nc.scalar.activation(tg[:], gains[:], ACT.Tanh).then_inc(s_tanh, 1)
            act.wait_ge(s_vset, 1)
            run_steps(step, act)

            def two(v, r, per=1):
                return v if r is None else r * (2 * per) + v

            def expert(e, r):
                p = e % 2
                act.wait_ge(p_eT, two(e + 1, r))
                if e >= 2:
                    act.wait_ge(p_H, two(4 * (e - 1), r, 4))
                nc.scalar.activation(xeT[p][:], S[:, p, :], ACT.Copy).then_inc(a_eT, 1)
                for f in (0, 2):
                    act.wait_ge(p_H, two(4 * e + f + 1, r, 4))
                    if e >= 2 and f == 0:
                        act.wait_ge(p_Y, two(e - 1, r))
                    nc.scalar.activation(hid[p][:, f, :], TS[:, f // 2, :], ACT.Relu, bias=b1s[p][:, f:f + 1]).then_inc(a_H, 1)

            expert(0, None)
            expert(1, None)
            with act.Fori(0, (E - 2) // 2) as r:
                for e in (2, 3):
                    expert(e, r)

        @block.vector
        def _(dve):
            V = nc.vector

            def fence(i):
                return V.tensor_tensor(fence_v[:, i:i + 1], ident[:, 0:1], ident[:, 0:1], ALU.mult)

            def top(n, q, r):
                dve.wait_ge(p_S, per_batch(4 * n + q + 1, r, 4))
                if n >= 2 and q == 0:
                    dve.wait_ge(v_m, per_batch(n - 1, r))
                V.tensor_reduce(negm[n % 2][:, 4 * q:4 * q + 4], S[:, q % 2, :].rearrange("p (h k) -> p h k", h=4),
                                AX.X, ALU.max, negate=True).then_inc(v_red, 1)

            def split_max(n, r):
                dve.wait_ge(v_red, per_batch(4 * n + 4, r, 4))
                if n >= 2:
                    dve.wait_ge(p_m, per_batch(n - 1, r))
                V.tensor_copy(mpart[n % 2][:, 0, :], negm[n % 2][:]).then_inc(v_m1, 1)
                dve.wait_ge(v_m1, per_batch(n + 1, r))
                V.tensor_tensor(mpart[n % 2][:, 1, :], negm[n % 2][:], mpart[n % 2][:, 0, :], ALU.subtract).then_inc(v_m, 1)

            def normalise(n, r):
                o = X[:, 1, :].rearrange("p (h v) -> p h v", v=HV)
                dve.wait_ge(p_back, per_batch(n + 1, r))
                if n >= 1:
                    dve.wait_ge(v_on, per_batch(n, r))
                V.reciprocal(rl[:], o[:, :, HD]).then_inc(v_rl, 1)
                dve.wait_ge(v_rl, per_batch(n + 1, r))
                if n >= 2:
                    dve.wait_ge(p_oT, per_batch(n - 1, r))
                V.tensor_tensor(on[n % 2][:].rearrange("p (h d) -> p h d", d=HD), o[:, :, 0:HD],
                                rl[:].unsqueeze(2).broadcast_to([P, HEADS, HD]), ALU.mult).then_inc(v_on, 1)

            def residual(n, r):
                dve.wait_ge(p_at, per_batch(n + 1, r))
                dve.wait_ge(g_xb, per_group(n // GB + 1, r))
                row = x_sb[:, bass.ds(per_batch(n, r), 1), :].rearrange("p o d -> p (o d)")
                V.tensor_tensor(row, X[:, 0, 0:D], row, ALU.add).then_inc(v_x1, 1)
                dve.wait_ge(v_x1, per_batch(n + 1, r))
                fence(0)
                V.bn_stats(st2[:, n % GB, :], row).then_inc(v_st2, 1)

            def moments2(G, r):
                dve.wait_ge(v_st2, per_batch(GB * G + GB, r))
                fence(1)
                for k in range(GB):
                    mm = V.bn_aggr(mv2[:, k, :], st2[:, k, :])
                mm.then_inc(v_mv2, 1)

            def normed2(G, r):
                dve.wait_ge(g_rs2, per_group(G + 1, r))
                dve.wait_ge(sent[G % 2], per_group(64 * (G // 2) + 64, r, 32))
                for k in range(GB):
                    row = x_sb[:, bass.ds(per_group(G * GB + k, r, GB), 1), :].rearrange("p o d -> p (o d)")
                    mm = V.tensor_scalar(rec[G % 2][:, k, 0:D], row, mv2[:, k, 0:1], rs2[:, 1, k:k + 1],
                                         ALU.subtract, ALU.mult)
                mm.then_inc(v_xn2, 1)

            def moments1(H, r):
                if H >= 1:
                    dve.wait_ge(v_xn, per_group(H, r))
                else:
                    dve.wait_ge(x_in[0], 16)
                if H in (1, 2):
                    dve.wait_ge(x_in[H], 16)
                fence(2)
                for k in range(GB):
                    row = x_sb[:, bass.ds(per_group(H * GB + k, r, GB), 1), :].rearrange("p o d -> p (o d)")
                    mm = V.bn_stats(st1[:, k, :], row)
                mm.then_inc(v_st1, 1)
                dve.wait_ge(v_st1, per_group(H + 1, r))
                fence(2)
                for k in range(GB):
                    mm = V.bn_aggr(mv1[:, k, :], st1[:, k, :])
                mm.then_inc(v_mv1, 1)

            def normed1(H, r):
                dve.wait_ge(g_rs1, per_group(H + 1, r))
                if H >= 1:
                    dve.wait_ge(p_xT, per_group(H, r))
                for k in range(GB):
                    row = x_sb[:, bass.ds(per_group(H * GB + k, r, GB), 1), :].rearrange("p o d -> p (o d)")
                    mm = V.tensor_scalar(xn[:, k, :], row, mv1[:, k, 0:1], rs1[:, 1, k:k + 1], ALU.subtract, ALU.mult)
                mm.then_inc(v_xn, 1)

            def value_rows(G, r):
                dve.wait_ge(p_v, per_group(G + 1, r))
                if G == 0:
                    dve.wait_ge(g_vals, 2)
                if G >= 2:
                    dve.wait_ge(p_O, per_batch(GB * (G - 2) + GB, r))
                V.tensor_tensor(vals[G % 2][:, :, :, 0:HD], X[:, 1, :].rearrange("p (k h d) -> p k h d", k=GB, d=HD),
                                bv[:].rearrange("p (h d) -> p h d", d=HD).unsqueeze(1).broadcast_to([P, GB, HEADS, HD]),
                                ALU.add).then_inc(v_v, 1)

            ROUTE = 6

            def route(G, r):
                def link(ins, i):
                    ins.then_inc(v_route, 1)
                    dve.wait_ge(v_route, per_group(ROUTE * G + i, r, ROUTE))

                dve.wait_ge(v_lg, per_group(G + 1, r))
                link(V.tensor_reduce(lmax[:], lgs[:], AX.X, ALU.max), 1)
                V.tensor_tensor(ldif[:], lgs[:], lmax[:].unsqueeze(2).broadcast_to([P, GB, E]), ALU.subtract).then_inc(v_ldif, 1)
                link(V.tensor_tensor(cand[:], lgs[:], lmax[:].unsqueeze(2).broadcast_to([P, GB, E]), ALU.is_lt), 2)
                link(V.scalar_tensor_tensor(cand[:], cand[:], float(E), iota, ALU.mult, ALU.add), 3)
                link(V.tensor_reduce(choice[:], cand[:], AX.X, ALU.min), 4)
                link(V.tensor_reduce(seen_g[:], mask[:].rearrange("p k e -> p e k"), AX.X, ALU.add), 5)
                link(V.tensor_tensor(seen[:], seen[:], seen_g[:], ALU.add), 6)
                V.tensor_tensor(mask[:], iota, choice[:].unsqueeze(2).broadcast_to([P, GB, E]), ALU.is_equal).then_inc(v_mask, 1)

            PLACE = 5

            def logits(G, r):
                dve.wait_ge(p_lg, per_group(G + 1, r))
                dve.wait_ge(v_xn2, per_group(G + 1, r))
                V.tensor_copy(lgs[:].rearrange("p k e -> p (k e)"), X[:, 1, 0:GB * E]).then_inc(v_lg, 1)

            def positions(G, r):
                dve.wait_ge(p_pos, per_group(G + 1, r))
                V.tensor_tensor(at_e[:].rearrange("p k e -> p (k e)"), X[:, 1, 0:GB * E],
                                mask[:].rearrange("p k e -> p (k e)"), ALU.mult).then_inc(v_pos, 1)

            def place(G, r):
                def link(ins, i):
                    ins.then_inc(v_place, 1)
                    dve.wait_ge(v_place, per_group(PLACE * G + i, r, PLACE))

                dve.wait_ge(v_pos, per_group(G + 1, r))
                dve.wait_ge(a_lexp, per_group(G + 1, r))
                V.tensor_reduce(lsum[:], lexp[:], AX.X, ALU.add)
                link(V.tensor_reduce(loc[:], at_e[:], AX.X, ALU.add), 1)
                V.tensor_scalar(over[:], loc[:], float(CAP), float(NONE), ALU.is_ge, ALU.mult)
                link(V.scalar_tensor_tensor(base[:], choice[:], float(CAP), loc[:], ALU.mult, ALU.add), 2)
                link(V.tensor_tensor(slot[G % 2][:], base[:], over[:], ALU.add), 3)
                link(V.reciprocal(rec[G % 2][:, :, 2 * D], lsum[:]), 4)
                link(V.tensor_copy(rec[G % 2][:, :, 2 * D + 1], token_code[:, bass.ds(per_group(G * GB, r, GB), GB)]), 5)
                fence(3).then_inc(v_slot, 1)

            def step(c, r):
                j, g = c % GB, c // GB
                if j == 1 and is_group(g - 2):
                    normed2(g - 2, r)
                if j == 2 and is_group(g + 2):
                    normed1(g + 2, r)
                if is_batch(c):
                    top(c, 0, r)
                if j == 0 and is_group(g):
                    value_rows(g, r)
                if is_batch(c):
                    top(c, 1, r)
                if is_batch(c - 4):
                    normalise(c - 4, r)
                if is_batch(c - 5):
                    residual(c - 5, r)
                if is_batch(c):
                    top(c, 2, r)
                if j == 1 and is_group(g + 2):
                    moments1(g + 2, r)
                if j == 2 and is_group(g - 2):
                    logits(g - 2, r)
                if j == 3 and is_group(g - 2):
                    positions(g - 2, r)
                if is_batch(c):
                    top(c, 3, r)
                    split_max(c, r)
                if j == 0 and is_group(g - 2):
                    moments2(g - 2, r)
                if j == 2 and is_group(g - 2):
                    route(g - 2, r)
                if j == 3 and is_group(g - 2):
                    place(g - 2, r)

            dve.wait_ge(s_cst, 16)
            V.tensor_copy(ident_b[:], ident)
            V.tensor_copy(before_b[:], cst[:, P:2 * P])
            V.memset(ones_b[:], 1.0)
            V.memset(mask[:], 0.0)
            V.memset(seen[:], 0.0)
            V.memset(ones_row[:], 1.0).then_inc(v_ones, 1)
            dve.wait_ge(s_wqkv, 16)
            dve.wait_ge(s_bias, 64)
            V.tensor_scalar(bq_s[:], bqk[:, 0:1], SCALE, None, ALU.mult)
            V.tensor_copy(wq_dh[:].rearrange("p (d h) -> p d h", h=HEADS), wqkv[:, 0:D].rearrange("p (h d) -> p d h", d=HD))
            V.tensor_copy(wk_dh[:].rearrange("p (d h) -> p d h", h=HEADS),
                          wqkv[:, D:2 * D].rearrange("p (h d) -> p d h", d=HD)).then_inc(s_vset, 1)

            for c in range(FIRST, LOOP0):
                if c == -4:
                    dve.wait_ge(s_late, 64)
                    dve.wait_ge(s_tanh, 1)
                    V.tensor_scalar(wout_g[:], wout[:], tg[:, 0:1], None, ALU.mult)
                    V.tensor_scalar(bout_g[:], bout[:], tg[:, 0:1], None, ALU.mult).then_inc(s_vset, 1)
                step(c, None)
            with dve.Fori(0, (LOOP1 - LOOP0) // BODY) as r:
                for c in range(LOOP0, LOOP0 + BODY):
                    step(c, r)
            for c in range(LOOP1, LAST + 1):
                step(c, None)

            def two(v, r, per=1):
                return v if r is None else r * (2 * per) + v

            def relus(e, r):
                p = e % 2
                for f in (1, 3):
                    dve.wait_ge(p_H, two(4 * e + f + 1, r, 4))
                    if e >= 2 and f == 1:
                        dve.wait_ge(p_Y, two(e - 1, r))
                    V.tensor_scalar(hid[p][:, f, :], O[:, f // 2, :], b1s[p][:, f:f + 1], 0.0, ALU.add, ALU.max).then_inc(v_H, 1)

            def finish(e, r):
                p = e % 2
                dve.wait_ge(e_in[p], two(16 * (e // 2) + 16, r, 8))
                if e >= 2:
                    dve.wait_ge(fin_out[p], two(64 * (e // 2), r, 32))
                V.tensor_scalar(gate2[p][:], xe[p][:, :, 2 * D], tg[:, 1:2], None, ALU.mult).then_inc(v_gate2, 1)
                V.tensor_scalar(tok[p][:], xe[p][:, :, 2 * D + 1], -1.0, float(NONE), ALU.mult, ALU.add).then_inc(v_tok, 1)
                dve.wait_ge(p_Y, two(e + 1, r))
                if e >= 1:
                    dve.wait_ge(v_fin, two(e, r))
                V.tensor_tensor(yb[:].rearrange("p (t n) -> p t n", n=D), X[:, p, :].rearrange("p (t n) -> p t n", n=D),
                                b2s[p][:].unsqueeze(1).broadcast_to([P, ET, D]), ALU.add).then_inc(v_yb, 1)
                dve.wait_ge(v_yb, two(e + 1, r))
                for t in range(ET):
                    mm = V.scalar_tensor_tensor(fin[p][:, t, :], yb[:, t * D:(t + 1) * D], gate2[p][:, t:t + 1],
                                                xe[p][:, t, D:2 * D], ALU.mult, ALU.add)
                mm.then_inc(v_fin, 1)

            relus(0, None)
            relus(1, None)
            finish(0, None)
            relus(2, None)
            finish(1, None)
            with dve.Fori(0, (E - 4) // 2) as r:
                for e in (3, 4):
                    relus(e, r)
                    finish(e - 1, r)
            relus(E - 1, None)
            finish(E - 2, None)
            finish(E - 1, None)

        @block.gpsimd
        def _(pool):
            G_ = nc.gpsimd

            def fence():
                return G_.tensor_tensor(fence_p[:], pool_c[:, 0, 0:1], pool_c[:, 0, 0:1], ALU.add).then_inc(g_fence, 1)

            def root(H, r, mv, rs, ready, e, done):
                pool.wait_ge(ready, per_group(H + 1, r))
                G_.tensor_tensor(rs[:, 0, :], mv[:, :, 1], pool_c[:, 0, :], ALU.add).then_inc(e, 1)
                pool.wait_ge(e, per_group(H + 1, r))
                G_.tensor_tensor(rs[:, 1, :], rs[:, 0, :], pool_c[:, 1, :], ALU.pow).then_inc(done, 1)

            def split(side, H, r):
                p, turn = H % 2, 2 * H + (0 if side == 1 else 1)
                pool.wait_ge((a_q, a_k)[side], per_group(H + 1, r))
                if H >= 1:
                    pool.wait_ge((g_q, g_k)[side], per_group(H, r))
                first = parts[side][p][:, 0, :]
                G_.tensor_tensor(rest[side][:], full[side][:], first, ALU.subtract)
                G_.tensor_tensor(parts[side][p][:, 1, :], full[side][:], first, ALU.subtract).then_inc(g_spl, 1)
                pool.wait_ge(g_spl, per_group(turn + 1, r, 2))
                G_.tensor_tensor(parts[side][p][:, 2, :], rest[side][:], parts[side][p][:, 1, :],
                                 ALU.subtract).then_inc((g_q, g_k)[side], 1)

            def scatter(G, r):
                p = G % 2
                if G == 0:
                    for q in sent:
                        pool.wait_ge(q, 64)
                pool.wait_ge(v_slot, per_group(G + 1, r))
                pool.wait_ge(a_rec, per_group(G + 1, r))
                fence()
                for k in range(GB):
                    G_.indirect_dma_start(rec_dram, bass.IndirectOffsetOnAxis(slot[p][:, k:k + 1], 0), rec[p][:, k, :], None,
                                          bounds_check=T - 1, oob_is_err=False).then_inc(sent[p], 16)

            def step(c, r):
                j, g = c % GB, c // GB
                if j == 0 and is_group(g - 2):
                    root(g - 2, r, mv2, rs2, v_mv2, g_e2, g_rs2)
                if j == 0 and is_group(g + 1):
                    split(1, g + 1, r)
                if j == 1 and is_group(g + 2):
                    root(g + 2, r, mv1, rs1, v_mv1, g_e1, g_rs1)
                if j == 1 and is_group(g + 1):
                    split(0, g + 1, r)
                if j == 2 and is_group(g + 1):
                    H = g + 1
                    pool.wait_ge(v_xn, per_group(H + 1, r))
                    if H <= 0:
                        pool.wait_ge(s_vset, 2)
                    rows = x_sb[:, bass.ds(per_group(H * GB, r, GB), GB), :]
                    G_.tensor_tensor(rows, rows, bout_g[:].unsqueeze(1).broadcast_to([P, GB, D]), ALU.add).then_inc(g_xb, 1)
                if j == 3 and is_group(g - 2):
                    scatter(g - 2, r)

            G_.memset(pool_c[:, 0, :], EPS)
            G_.memset(pool_c[:, 1, :], -0.5).then_inc(s_pset, 1)
            for i in range(2):
                G_.memset(vals[i][:, :, :, HD:HV], 0.0).then_inc(g_zero, 1)
            pool.wait_ge(g_zero, 2)
            for i in range(2):
                G_.memset(vals[i][:, :, :, HD:HD + 1], 1.0).then_inc(g_vals, 1)
            G_.memset(zeros[:], 0.0).then_inc(s_zero, 1)
            pool.wait_ge(s_pset, 1)
            pool.wait_ge(s_zero, 1)
            for i in range(8):
                pool.dma_start(rec_dram[i * (T // 8):(i + 1) * (T // 8), :].rearrange("(p a) c -> p (a c)", p=P),
                               zeros[:]).then_inc(sent[i % 2], 16)
            run_steps(step, pool)

            def rows_out(e, r):
                p = e % 2
                pool.wait_ge(v_fin, e + 1 if r is None else r * 2 + (e + 1))
                pool.wait_ge(v_tok, e + 1 if r is None else r * 2 + (e + 1))
                pool.wait_ge(g_fence, r * 2 + (NG + e))
                fence()
                for t in range(ET):
                    G_.indirect_dma_start(out_rows, bass.IndirectOffsetOnAxis(tok[p][:, t:t + 1], 0), fin[p][:, t, :], None,
                                          bounds_check=T - 1, oob_is_err=False).then_inc(fin_out[p], 16)

            pool.wait_ge(x1_out, 16 * NG)
            with pool.Fori(0, E // 2) as r:
                for e in (0, 1):
                    rows_out(e, r)


_INS = ['x', 'ctx_1024', 'g_xattn', 'g_ffn', 'L0_xattn_W_qkv', 'L0_xattn_b_qkv', 'L0_xattn_W_out', 'L0_xattn_b_out',
        'L0_ffn_Wg', 'L0_ffn_W1', 'L0_ffn_b1', 'L0_ffn_W2', 'L0_ffn_b2']


def kernel(**inputs):
    import numpy as _np
    import concourse.bacc as _bacc
    from concourse import mybir as _mybir
    from concourse.bass_utils import run_bass_kernel_spmd as _run

    nc = _bacc.Bacc("TRN2", target_bir_lowering=False, num_devices=1)
    arrays, args = {}, []
    for name in _INS:
        a = _np.ascontiguousarray(inputs[name])
        arrays[f"in_{name}_dram"] = a
        args.append(nc.dram_tensor(f"in_{name}_dram", a.shape, _mybir.dt.from_np(a.dtype), kind="ExternalInput").ap())
    n_b, n_e, n_k = inputs['x'].shape[0], inputs['L0_ffn_Wg'].shape[1], GB
    tokens = _np.arange(n_b * P, dtype=_np.float32).reshape(n_b, P).T
    consts = _np.concatenate([_np.eye(P), _np.triu(_np.ones((P, P)), 1),
                              _np.tile(_np.arange(n_e), (P, n_k)), 2 * n_b * P - tokens], axis=1).astype(_np.float32)
    arrays["in_consts_dram"] = consts
    args.append(nc.dram_tensor("in_consts_dram", consts.shape, _mybir.dt.float32, kind="ExternalInput").ap())
    shape = tuple(inputs['x'].shape)
    args.append(nc.dram_tensor("out_0_dram", shape, _mybir.dt.float32, kind="ExternalOutput").ap())
    flamingo_kernel(nc, *args)
    r = _run(nc, [arrays], core_ids=[0])
    return r.results[0]["out_0_dram"]
```

```python
from contextlib import ExitStack

import concourse.bass as bass
from concourse import mybir

F32 = mybir.dt.float32
BF16 = mybir.dt.bfloat16
U32 = mybir.dt.uint32
ALU = mybir.AluOpType
ACT = mybir.ActivationFunctionType
AX = mybir.AxisListType

P = 128
GB = 4
BODY = 8
EPS = 1e-5
Q_PARTS = (0, 0, 0, 1, 1, 2)
K_PARTS = (0, 1, 2, 0, 1, 0)
REC = 2 * P + 2


def flamingo_kernel(nc, x, ctx_in, g_xattn, g_ffn, w_qkv, b_qkv, w_out, b_out, wg, w1, b1, w2, b2, consts, out):
    B, L, D = x.shape
    E, _, F = w1.shape
    T = B * L
    CAP = -(-T // E)
    HEADS = 16
    HD = D // HEADS
    HV = 32
    SCALE = float(HD) ** -0.5
    NG = B // GB
    GT = GB * L
    SLOTS = len(Q_PARTS)
    KR = SLOTS * HD
    KM = KR + 2
    FC = F // P
    ET = CAP // P
    NONE = 2 * T
    LOOP0, LOOP1 = BODY, B - BODY
    FIRST, LAST = -8, 4 * (NG - 1) + 11
    assert L == P and D == P and CAP == 4 * P and F == 4 * P and E == 8

    with ExitStack() as ctx:
        def sb(name, shape, dt=F32):
            return ctx.enter_context(nc.sbuf_tensor(name, shape, dt))

        def ps(name):
            return ctx.enter_context(nc.psum_tensor(name, [P, 2, 512], F32))

        def sem(name):
            return ctx.enter_context(nc.semaphore(name))

        def sem2(name):
            return [sem(name + "0"), sem(name + "1")]

        rec_dram = nc.dram_tensor("rec_dram", (T, REC), F32).ap()

        S = ps("S")
        TS = ps("TS")
        O = ps("O")
        X = ps("X")

        cst = sb("cst", [P, 2 * P + GB * E + B])
        ident = cst[:, 0:P]
        iota = cst[:, 2 * P:2 * P + GB * E].rearrange("p (k e) -> p k e", e=E)
        token_code = cst[:, 2 * P + GB * E:]
        ident_b = sb("ident_b", [P, P], BF16)
        before_b = sb("before_b", [P, P], BF16)
        ones_b = sb("ones_b", [P, P], BF16)
        wqkv = sb("wqkv", [P, 3 * D])
        wq_dh = sb("wq_dh", [P, D])
        wk_dh = sb("wk_dh", [P, D])
        bqk = sb("bqk", [P, 2])
        bq_s = sb("bq_s", [P, 1])
        bv = sb("bv", [P, D])
        wout = sb("wout", [P, D])
        wout_g = sb("wout_g", [P, D])
        bout = sb("bout", [P, D])
        bout_g = sb("bout_g", [P, D])
        wg_sb = sb("wg_sb", [P, E])
        gains = sb("gains", [P, 2])
        tg = sb("tg", [P, 2])
        pool_c = sb("pool_c", [P, 3, GB])
        zeros = sb("zeros", [P, REC])
        fence_v = sb("fence_v", [P, 4])
        fence_p = sb("fence_p", [P, 1])

        x_sb = sb("x_sb", [P, B, D])
        c_sb = [sb(f"c_sb{i}", [P, GB, D]) for i in range(2)]
        cT = [sb(f"cT{i}", [P, GT]) for i in range(2)]
        xn = sb("xn", [P, GB, D])
        xnT = sb("xnT", [P, GT])
        st1 = sb("st1", [P, GB, 6])
        mv1 = sb("mv1", [P, GB, 2])
        rs1 = sb("rs1", [P, 4, GB])
        full = [sb(f"full_{s}", [P, GT]) for s in "qk"]
        rest = [sb(f"rest_{s}", [P, GT]) for s in "qk"]
        parts = [[sb(f"parts_{s}{i}", [P, 3, GT], BF16) for i in range(2)] for s in "qk"]
        qp = [sb(f"qp{i}", [P, HEADS, GT], BF16) for i in range(2)]
        kp = [sb(f"kp{i}", [P, HEADS, GT], BF16) for i in range(2)]
        vals = [sb(f"vals{i}", [P, GB, HEADS, HV]) for i in range(2)]
        ones_row = sb("ones_row", [2 * HEADS, GT], BF16)
        oraw = [sb(f"oraw{i}", [P, 4 * L]) for i in range(2)]
        negm = [sb(f"negm{i}", [P, HEADS]) for i in range(2)]
        mpart = [sb(f"mpart{i}", [P, 2, HEADS], BF16) for i in range(2)]
        mrow = [sb(f"mrow{i}", [2 * HEADS, P], BF16) for i in range(2)]
        prob = [sb(f"prob{i}", [P, HEADS * L]) for i in range(2)]
        rl = sb("rl", [P, HEADS])
        on = [sb(f"on{i}", [P, D]) for i in range(2)]
        onT = [sb(f"onT{i}", [P, L]) for i in range(2)]
        st2 = sb("st2", [P, GB, 6])
        mv2 = sb("mv2", [P, GB, 2])
        rs2 = sb("rs2", [P, 4, GB])
        rec = [sb(f"rec{i}", [P, GB, REC]) for i in range(2)]
        xn2T = sb("xn2T", [P, GT])
        lgs = sb("lgs", [P, GB, E])
        lmax = sb("lmax", [P, GB])
        ldif = sb("ldif", [P, GB, E])
        lexp = sb("lexp", [P, GB, E])
        lsum = sb("lsum", [P, GB])
        cand = sb("cand", [P, GB, E])
        choice = sb("choice", [P, GB])
        mask = sb("mask", [P, GB, E], BF16)
        seen = sb("seen", [P, E], BF16)
        seen_g = sb("seen_g", [P, E])
        at_e = sb("at_e", [P, GB, E])
        loc = sb("loc", [P, GB])
        over = sb("over", [P, GB])
        base = sb("base", [P, GB])
        slot = [sb(f"slot{i}", [P, GB], U32) for i in range(2)]
        w1s = [sb(f"w1s{i}", [P, F]) for i in range(2)]
        w2s = [sb(f"w2s{i}", [P, FC, D]) for i in range(2)]
        b1_all = sb("b1_all", [P, E, FC])
        b2_all = sb("b2_all", [P, E, D])
        b1_act = [sb(f"b1_act{i}", [P, 1, FC]) for i in range(2)]
        b1_dve = [sb(f"b1_dve{i}", [P, 1, FC]) for i in range(2)]
        xe = [sb(f"xe{i}", [P, ET, D]) for i in range(2)]
        xr = [sb(f"xr{i}", [P, ET, REC - D]) for i in range(2)]
        xeT = [sb(f"xeT{i}", [P, CAP]) for i in range(2)]
        hid = [qp[i][:, 0:8, :].rearrange("p h n -> p (h n)").bitcast(F32).rearrange("p (f n) -> p f n", f=FC)
               for i in range(2)]
        yb = sb("yb", [P, CAP])
        gate2 = [sb(f"gate2_{i}", [P, ET]) for i in range(2)]
        tok = [sb(f"tok{i}", [P, ET], U32) for i in range(2)]
        fin = [sb(f"fin{i}", [P, ET, D]) for i in range(2)]

        s_cst, s_wqkv, s_bias, s_late = sem("s_cst"), sem("s_wqkv"), sem("s_bias"), sem("s_late")
        s_zero, s_vset, s_tanh, s_pset = sem("s_zero"), sem("s_vset"), sem("s_tanh"), sem("s_pset")
        x_in = [sem(f"x_in{i}") for i in range(3)]
        c_in, q_in, k_in, m_in = sem2("c_in"), sem2("q_in"), sem2("k_in"), sem2("m_in")
        x1_out, sent = sem("x1_out"), sem2("sent")
        p_cT, p_xT, p_q, p_k, p_v = sem("p_cT"), sem("p_xT"), sem("p_q"), sem("p_k"), sem("p_v")
        g_zero = sem("g_zero")
        v_ones, g_vals = sem("v_ones"), sem("g_vals")
        p_back, a_O, s_ones = sem("p_back"), sem("a_O"), sem("s_ones")
        p_S, p_m, p_T, p_O, p_oT, p_at = sem("p_S"), sem("p_m"), sem("p_T"), sem("p_O"), sem("p_oT"), sem("p_at")
        p_nT, p_lg, p_pos = sem("p_nT"), sem("p_lg"), sem("p_pos")
        a_cT, a_xT, a_q, a_k, a_m = sem("a_cT"), sem("a_xT"), sem("a_q"), sem("a_k"), sem("a_m")
        a_exp, a_oT, a_nT, a_lexp = sem("a_exp"), sem("a_oT"), sem("a_nT"), sem("a_lexp")
        v_st1, v_mv1, v_xn, v_v, v_red, v_m1, v_m = (sem("v_st1"), sem("v_mv1"), sem("v_xn"), sem("v_v"), sem("v_red"),
                                                     sem("v_m1"), sem("v_m"))
        v_rl, v_on, v_x1, v_st2, v_mv2, a_xn2 = sem("v_rl"), sem("v_on"), sem("v_x1"), sem("v_st2"), sem("v_mv2"), sem("a_xn2")
        v_lg, v_ldif, v_route, v_mask, v_pos, v_place, v_slot = (sem("v_lg"), sem("v_ldif"), sem("v_route"), sem("v_mask"),
                                                                sem("v_pos"), sem("v_place"), sem("v_slot"))
        g_e1, g_rs1, g_e2, g_rs2, g_xb, g_spl, g_q, g_k = (sem("g_e1"), sem("g_rs1"), sem("g_e2"), sem("g_rs2"), sem("g_xb"),
                                                           sem("g_spl"), sem("g_q"), sem("g_k"))
        g_fence = sem("g_fence")
        w1_in, w2_in, xe_in, xr_in, fin_out = sem2("w1_in"), sem2("w2_in"), sem2("xe_in"), sem2("xr_in"), sem2("fin_out")
        b12_in, v_b1 = sem("b12_in"), sem("v_b1")
        p_eT, p_H, p_Y = sem("p_eT"), sem("p_H"), sem("p_Y")
        a_eT, a_H, v_H, v_yb, v_gate2, v_tok, v_fin = (sem("a_eT"), sem("a_H"), sem("v_H"), sem("v_yb"), sem("v_gate2"),
                                                       sem("v_tok"), sem("v_fin"))

        x_v = x.rearrange("b p d -> p b d")
        out_v = out.rearrange("b p d -> p b d")
        out_rows = out.rearrange("b p d -> (b p) d")
        ctx_v = ctx_in.rearrange("b p d -> p b d")
        rec_v = rec_dram.rearrange("(e t p) c -> e p t c", t=ET, p=P)

        def per_batch(v, r, per=1):
            return v if r is None else r * (per * BODY) + v

        def per_group(v, r, per=1):
            return v if r is None else r * (per * BODY // GB) + v

        def is_batch(n):
            return 0 <= n < B

        def is_group(g):
            return 0 <= g < NG

        BATCH_TASKS = ("m", "at", "back", "oT")

        def x_tasks(c):
            j, g = c % GB, c // GB
            first = {0: ("v", g), 2: ("cT", g + 2), 3: ("k", g + 2)}.get(j)
            third = {2: ("lg", g - 2), 3: ("pos", g - 2)}.get(j)
            second = {1: ("nT", g - 2), 2: ("xT", g + 2), 3: ("q", g + 2)}.get(j)
            bank0 = [("m", c - 1), ("at", c - 5), second]
            bank1 = [first, ("back", c - 4), third, ("oT", c - 4)]
            ok = lambda t: t is not None and (is_batch(t[1]) if t[0] in BATCH_TASKS else is_group(t[1]))
            return [[t for t in bank0 if ok(t)], [t for t in bank1 if ok(t)]]

        before = {}
        for bank in range(2):
            last = None
            for c in range(FIRST, LAST + 1):
                for t in x_tasks(c)[bank]:
                    before[t] = last
                    last = t
        emptied = {"v": v_v, "cT": a_cT, "k": a_k, "lg": v_lg, "pos": v_pos, "nT": a_nT, "xT": a_xT, "q": a_q,
                   "m": a_m, "at": v_x1, "back": v_on, "oT": a_oT}

        def bank_free(eng, name, idx, r):
            t = before[(name, idx)]
            if t is not None:
                step = per_batch if t[0] in BATCH_TASKS else per_group
                eng.wait_ge(emptied[t[0]], step(t[1] + 1, r))

        def run_steps(step_fn, eng):
            for c in range(FIRST, LOOP0):
                step_fn(c, None)
            with eng.Fori(0, (LOOP1 - LOOP0) // BODY) as r:
                for c in range(LOOP0, LOOP0 + BODY):
                    step_fn(c, r)
            for c in range(LOOP1, LAST + 1):
                step_fn(c, None)

        block = ctx.enter_context(nc.Block())

        @block.sync
        def _(sp):
            sp.dma_start(x_sb[:, 0:GB, :], x_v[:, 0:GB, :]).then_inc(x_in[0], 16)
            sp.dma_start(cst[:], consts).then_inc(s_cst, 16)
            sp.dma_start(wqkv[:], w_qkv).then_inc(s_wqkv, 16)
            for i in range(2):
                sp.dma_start(bqk[:, i:i + 1], b_qkv[i * D:(i + 1) * D].rearrange("(h d o) -> d h o", d=HD, o=1),
                             allow_slow_non_contiguous=True).then_inc(s_bias, 16)
            sp.dma_start(gains[:, 0:1], g_xattn.rearrange("(a n) -> a n", a=1).broadcast_to([P, 1])).then_inc(s_bias, 16)
            sp.dma_start(gains[:, 1:2], g_ffn.rearrange("(a n) -> a n", a=1).broadcast_to([P, 1])).then_inc(s_bias, 16)

            def moved(view, offset):
                return view if offset is None else bass.AP(view.tensor, offset, view.ap)

            def load_w1(e, at):
                sp.dma_start(w1s[e % 2][:], moved(w1[e % 2], at)).then_inc(w1_in[e % 2], 16)

            def load_w2(e, at):
                sp.dma_start(w2s[e % 2][:], moved(w2[e % 2].rearrange("(f p) n -> p f n", p=P), at)).then_inc(w2_in[e % 2], 16)

            scratch = sp.alloc_register("ready")

            def ready(*values):
                for v in values:
                    if not isinstance(v, int):
                        sp.reg_mov(scratch, v)

            def late_loads():
                sp.dma_start(x_sb[:, GB:2 * GB, :], x_v[:, GB:2 * GB, :]).then_inc(x_in[1], 16)
                sp.dma_start(bv[:], b_qkv[2 * D:3 * D].rearrange("(a n) -> a n", a=1).broadcast_to([P, D])).then_inc(s_late, 16)
                sp.dma_start(bout[:], b_out.rearrange("(a n) -> a n", a=1).broadcast_to([P, D])).then_inc(s_late, 16)
                sp.dma_start(wout[:], w_out).then_inc(s_late, 16)
                sp.dma_start(wg_sb[:], wg).then_inc(s_late, 16)

            def step(c, r):
                j, g = c % GB, c // GB
                loads, stores = j == 0 and is_group(g + 2), j == 0 and is_group(g - 2)
                if j == 0:
                    ready(per_batch(c, r), per_group(g + 1, r), per_batch(GB * (g - 2) + GB, r))
                if is_batch(c - 1):
                    sp.wait_ge(a_m, per_batch(c, r))
                if loads and g + 2 >= 2:
                    sp.wait_ge(p_cT, per_group(g + 1, r))
                if is_batch(c - 1):
                    n, p = c - 1, (c - 1) % 2
                    G = n // GB
                    t0 = (n % GB) * L
                    sp.dma_start(qp[G % 2][KR:KM, :, t0:t0 + L], mrow[p][:]).then_inc(m_in[p], 16)
                if loads:
                    sp.dma_start(c_sb[g % 2][:], ctx_v[:, bass.ds(per_group((g + 2) * GB, r, GB), GB), :]).then_inc(c_in[g % 2], 16)
                if stores:
                    sp.wait_ge(v_x1, per_batch(GB * (g - 2) + GB, r))
                    sl = bass.ds(per_group((g - 2) * GB, r, GB), GB)
                    sp.dma_start(out_v[:, sl, :], rec[g % 2][:, :, D:2 * D]).then_inc(x1_out, 16)
                if is_group(g + 1) and j in (2, 3):
                    H, p = g + 1, (g + 1) % 2
                    if j == 2:
                        ready(per_batch(4 * (GB * H - 5) + 4, r, 4), per_group(H + 1, r))
                        if H >= 2:
                            sp.wait_ge(p_T, per_batch(4 * (GB * H - 5) + 4, r, 4))
                        sp.wait_ge(g_k, per_group(H + 1, r))
                        sp.wait_ge(a_k, per_group(H + 1, r))
                    pieces = [("k", s) for s in range(SLOTS)] + [("q", s) for s in range(SLOTS)]
                    for side, s in (pieces[:8] if j == 2 else pieces[8:]):
                        if (side, s) == ("q", 0):
                            sp.wait_ge(g_q, per_group(H + 1, r))
                            sp.wait_ge(a_q, per_group(H + 1, r))
                        dst = (kp if side == "k" else qp)[p][s * HD:(s + 1) * HD, :, :]
                        src = parts[side == "k"][p][:, (K_PARTS if side == "k" else Q_PARTS)[s], :]
                        sp.dma_start(dst, src).then_inc((k_in if side == "k" else q_in)[p], 16)
                if c == -8:
                    late_loads()
                if c == 0:
                    sp.dma_start(x_sb[:, 2 * GB:, :], x_v[:, 2 * GB:, :]).then_inc(x_in[2], 16)
                if c == -1:
                    sp.wait_ge(v_ones, 1)
                    for i in range(2):
                        sp.dma_start(kp[i][KR:KM, :, :], ones_row[:]).then_inc(s_ones, 16)
                if c == 2:
                    for e in range(2):
                        load_w1(e, None)
                        load_w2(e, None)
                    sp.dma_start(b1_all[:], b1.rearrange("e (f p) -> p e f", p=P),
                                 allow_slow_non_contiguous=True).then_inc(b12_in, 16)
                    sp.dma_start(b2_all[:], b2.rearrange("(a e) n -> a (e n)", a=1).broadcast_to([P, E * D])).then_inc(b12_in, 16)

            run_steps(step, sp)

            def load_xe(e, at):
                sp.dma_start(xe[e % 2][:], moved(rec_v[e % 2][:, :, 0:D], at)).then_inc(xe_in[e % 2], 16)

            def load_xr(e, at):
                sp.dma_start(xr[e % 2][:], moved(rec_v[e % 2][:, :, D:REC], at)).then_inc(xr_in[e % 2], 16)

            for p in range(2):
                sp.wait_ge(sent[p], 16 + 16 * GB * (NG // 2))
            for e in range(2):
                load_xe(e, None)
            for e in range(2):
                load_xr(e, None)
            with sp.Fori(0, (E - 2) // 2) as r:
                for e in (2, 3):
                    w_at, xe_at = r * (2 * D * F) + e * D * F, r * (2 * CAP * REC) + e * CAP * REC
                    xr_at = r * (2 * CAP * REC) + (e * CAP * REC + D)
                    turned, used, through = r * 2 + (e - 1), r * 8 + 4 * (e - 1), r * 2 + (e - 1)
                    ready(w_at * 4, xe_at * 4, xr_at * 4, turned, used, through)
                    sp.wait_ge(p_eT, turned)
                    load_xe(e, xe_at)
                    sp.wait_ge(p_H, used)
                    load_w1(e, w_at)
                    sp.wait_ge(p_Y, through)
                    load_w2(e, w_at)
                    sp.wait_ge(v_fin, through)
                    load_xr(e, xr_at)
            sp.wait_ge(x1_out, 16 * NG)
            for p in range(2):
                sp.wait_ge(fin_out[p], 16 * ET * (E // 2))

        @block.tensor
        def _(pe):
            def group_task(name, idx, r):
                bank_free(pe, name, idx, r)
                if name == "cT":
                    pe.wait_ge(c_in[idx % 2], per_group(16 * (idx // 2) + 16, r, 8))
                    if idx == 0:
                        pe.wait_ge(s_cst, 16)
                    for k in range(GB):
                        mm = nc.tensor.transpose(X[:, 1, k * L:(k + 1) * L], c_sb[idx % 2][:, k, :], ident)
                    mm.then_inc(p_cT, 1)
                elif name == "xT":
                    pe.wait_ge(v_xn, per_group(idx + 1, r))
                    for k in range(GB):
                        mm = nc.tensor.transpose(X[:, 0, k * L:(k + 1) * L], xn[:, k, :], ident)
                    mm.then_inc(p_xT, 1)
                elif name == "k":
                    pe.wait_ge(a_cT, per_group(idx + 1, r))
                    if idx == 0:
                        pe.wait_ge(s_vset, 1)
                    nc.tensor.matmul(X[:, 1, :], wk_dh[:], cT[idx % 2][:], start=True, stop=True).then_inc(p_k, 1)
                elif name == "q":
                    pe.wait_ge(a_xT, per_group(idx + 1, r))
                    nc.tensor.matmul(X[:, 0, :], wq_dh[:], xnT[:], start=True, stop=True).then_inc(p_q, 1)
                elif name == "v":
                    for k in range(GB):
                        mm = nc.tensor.matmul(X[:, 1, k * L:(k + 1) * L], cT[idx % 2][:, k * L:(k + 1) * L],
                                              wqkv[:, 2 * D:3 * D], start=True, stop=True)
                    mm.then_inc(p_v, 1)
                elif name == "nT":
                    pe.wait_ge(a_xn2, per_group(idx + 1, r))
                    for k in range(GB):
                        mm = nc.tensor.transpose(X[:, 0, k * L:(k + 1) * L], rec[idx % 2][:, k, 0:D], ident)
                    mm.then_inc(p_nT, 1)
                elif name == "lg":
                    pe.wait_ge(a_nT, per_group(idx + 1, r))
                    for k in range(GB):
                        mm = nc.tensor.matmul(X[:, 1, k * E:(k + 1) * E], xn2T[:, k * L:(k + 1) * L], wg_sb[:],
                                              start=True, stop=True)
                    mm.then_inc(p_lg, 1)
                elif name == "pos":
                    pe.wait_ge(v_mask, per_group(idx + 1, r))
                    for k in range(GB):
                        o = X[:, 1, k * E:(k + 1) * E]
                        nc.tensor.matmul(o, before_b[:], mask[:, k, :], start=True, stop=False)
                        for k2 in range(k):
                            nc.tensor.matmul(o, ones_b[:], mask[:, k2, :], start=False, stop=False)
                        mm = nc.tensor.matmul(o, ones_b[:], seen[:], start=False, stop=True)
                    mm.then_inc(p_pos, 1)

            def scores(n, q, r):
                G, t0 = n // GB, (n % GB) * L
                if q == 0 and n % GB == 0:
                    pe.wait_ge(q_in[G % 2], per_group(96 * (G // 2) + 96, r, 48))
                    pe.wait_ge(k_in[G % 2], per_group(96 * (G // 2) + 96, r, 48))
                if 4 * n + q >= 2:
                    pe.wait_ge(v_red, per_batch(4 * n + q - 1, r, 4))
                for h in range(4 * q, 4 * q + 4):
                    o = (h % 4) * L
                    mm = nc.tensor.matmul(S[:, q % 2, o:o + L], qp[G % 2][0:KR, h, t0:t0 + L],
                                          kp[G % 2][0:KR, h, t0:t0 + L], start=True, stop=True)
                mm.then_inc(p_S, 1)

            def shifted(n, q, r):
                G, t0 = n // GB, (n % GB) * L
                if q == 0:
                    if n == 0:
                        pe.wait_ge(s_ones, 32)
                    pe.wait_ge(m_in[n % 2], per_batch(16 * (n // 2) + 16, r, 8))
                if 4 * n + q >= 2:
                    pe.wait_ge(a_exp, per_batch(4 * n + q - 1, r, 4))
                for h in range(4 * q, 4 * q + 4):
                    o = (h % 4) * L
                    mm = nc.tensor.matmul(TS[:, q % 2, o:o + L], kp[G % 2][0:KM, h, t0:t0 + L],
                                          qp[G % 2][0:KM, h, t0:t0 + L], start=True, stop=True)
                mm.then_inc(p_T, 1)

            def values(n, q, r):
                G, k = n // GB, n % GB
                pe.wait_ge(a_exp, per_batch(4 * n + q + 1, r, 4))
                if q == 0:
                    if k == 0:
                        pe.wait_ge(v_v, per_group(G + 1, r))
                    if n >= 2:
                        pe.wait_ge(a_O, per_batch(n - 1, r))
                for h in range(4 * q, 4 * q + 4):
                    i = h % 4
                    mm = nc.tensor.matmul(O[i * HV:(i + 1) * HV, n % 2, q * L:(q + 1) * L], vals[G % 2][:, k, h, :],
                                          prob[n % 2][:, h * L:(h + 1) * L], start=True, stop=True)
                if q == 3:
                    mm.then_inc(p_O, 1)

            def step(c, r):
                todo = x_tasks(c)
                groups = [t for bank in todo for t in bank if t[0] not in BATCH_TASKS]
                at_q = {0: [t for t in groups if t[0] in ("v", "cT", "k")], 1: [],
                        2: [t for t in groups if t[0] in ("lg", "pos", "nT", "xT", "q")], 3: []}
                for q in range(4):
                    if is_batch(c):
                        scores(c, q, r)
                    if is_batch(c - 2):
                        shifted(c - 2, q, r)
                    if q == 0 and is_batch(c - 1):
                        bank_free(pe, "m", c - 1, r)
                        pe.wait_ge(v_m, per_batch(c, r))
                        nc.tensor.transpose(X[:, 0, 0:P // 2].bitcast(BF16)[0:2 * HEADS, :],
                                            mpart[(c - 1) % 2][:].rearrange("p j h -> p (j h)"), ident_b[:]).then_inc(p_m, 1)
                    for t in at_q[q]:
                        group_task(t[0], t[1], r)
                    if q == 1 and is_batch(c - 5):
                        bank_free(pe, "at", c - 5, r)
                        pe.wait_ge(a_oT, per_batch(c - 4, r))
                        nc.tensor.matmul(X[:, 0, 0:D], onT[(c - 5) % 2][:], wout_g[:], start=True, stop=True).then_inc(p_at, 1)
                    if q == 1 and is_batch(c - 4):
                        bank_free(pe, "back", c - 4, r)
                        pe.wait_ge(a_O, per_batch(c - 3, r))
                        for i in range(4):
                            mm = nc.tensor.transpose(X[:, 1, i * L:(i + 1) * L], oraw[c % 2][:, i * L:(i + 1) * L], ident)
                        mm.then_inc(p_back, 1)
                    if q == 3 and is_batch(c - 4):
                        bank_free(pe, "oT", c - 4, r)
                        pe.wait_ge(v_on, per_batch(c - 3, r))
                        nc.tensor.transpose(X[:, 1, 0:L], on[c % 2][:], ident).then_inc(p_oT, 1)
                    if is_batch(c - 3):
                        values(c - 3, q, r)

            run_steps(step, pe)

            def two(v, r, per=1):
                return v if r is None else r * (2 * per) + v

            def turn(e, r):
                pe.wait_ge(xe_in[e % 2], two(16 * (e // 2) + 16, r, 8))
                if e >= 2:
                    pe.wait_ge(a_eT, two(e - 1, r))
                for t in range(ET):
                    mm = nc.tensor.transpose(S[:, e % 2, t * P:(t + 1) * P], xe[e % 2][:, t, 0:D], ident)
                mm.then_inc(p_eT, 1)

            def hidden(e, r):
                pe.wait_ge(a_eT, two(e + 1, r))
                pe.wait_ge(w1_in[e % 2], two(16 * (e // 2) + 16, r, 8))
                for f in range(FC):
                    if e >= 1:
                        pe.wait_ge(a_H if f % 2 == 0 else v_H, two(2 * (e - 1) + f // 2 + 1, r, 2))
                    bank = (TS if f % 2 == 0 else O)[:, f // 2, :]
                    nc.tensor.matmul(bank, w1s[e % 2][:, f * P:(f + 1) * P], xeT[e % 2][:], start=True, stop=True).then_inc(p_H, 1)

            def outputs(e, r):
                pe.wait_ge(a_H, two(2 * e + 2, r, 2))
                pe.wait_ge(v_H, two(2 * e + 2, r, 2))
                pe.wait_ge(w2_in[e % 2], two(16 * (e // 2) + 16, r, 8))
                if e >= 2:
                    pe.wait_ge(v_yb, two(e - 1, r))
                for t in range(ET):
                    for f in range(FC):
                        mm = nc.tensor.matmul(X[:, e % 2, t * P:(t + 1) * P], hid[e % 2][:, f, t * P:(t + 1) * P],
                                              w2s[e % 2][:, f, :], start=(f == 0), stop=(f == FC - 1))
                mm.then_inc(p_Y, 1)

            turn(0, None)
            hidden(0, None)
            turn(1, None)
            hidden(1, None)
            outputs(0, None)
            turn(2, None)
            hidden(2, None)
            outputs(1, None)
            with pe.Fori(0, (E - 4) // 2) as r:
                for e in (3, 4):
                    turn(e, r)
                    hidden(e, r)
                    outputs(e - 1, r)
            turn(E - 1, None)
            hidden(E - 1, None)
            outputs(E - 2, None)
            outputs(E - 1, None)

        @block.scalar
        def _(act):
            def proj(side, H, r):
                ready, done, bank = ((p_q, a_q, 0), (p_k, a_k, 1))[side]
                act.wait_ge(ready, per_group(H + 1, r))
                if H >= 1:
                    act.wait_ge((g_q, g_k)[side], per_group(H, r))
                if H >= 2:
                    act.wait_ge((q_in, k_in)[side][H % 2], per_group(96 * (H // 2), r, 48))
                bias = bq_s[:, 0:1] if side == 0 else bqk[:, 1:2]
                sc = SCALE if side == 0 else 1.0
                nc.scalar.activation(full[side][:], X[:, bank, :], ACT.Identity, bias=bias, scale=sc)
                nc.scalar.activation(parts[side][H % 2][:, 0, :], X[:, bank, :], ACT.Identity, bias=bias,
                                     scale=sc).then_inc(done, 1)

            def exps(n, q, r):
                act.wait_ge(p_T, per_batch(4 * n + q + 1, r, 4))
                if n >= 2:
                    if q == 0:
                        act.wait_ge(p_O, per_batch(n - 1, r))
                nc.scalar.activation(prob[n % 2][:, q * 512:(q + 1) * 512], TS[:, q % 2, :], ACT.Exp).then_inc(a_exp, 1)

            def step(c, r):
                j, g = c % GB, c // GB
                if is_batch(c - 1):
                    n = c - 1
                    act.wait_ge(p_m, per_batch(n + 1, r))
                    if n >= 2:
                        act.wait_ge(m_in[n % 2], per_batch(16 * (n // 2), r, 8))
                    nc.scalar.activation(mrow[n % 2][:], X[:, 0, 0:P // 2].bitcast(BF16)[0:2 * HEADS, :],
                                         ACT.Copy).then_inc(a_m, 1)
                if is_batch(c - 4):
                    n = c - 4
                    act.wait_ge(p_O, per_batch(n + 1, r))
                    if n >= 2:
                        act.wait_ge(p_back, per_batch(n - 1, r))
                    nc.scalar.activation(oraw[n % 2][:], O[:, n % 2, :], ACT.Copy).then_inc(a_O, 1)
                if is_batch(c - 2):
                    exps(c - 2, 0, r)
                if j == 1 and is_group(g - 2):
                    G = g - 2
                    act.wait_ge(g_rs2, per_group(G + 1, r))
                    for k in range(GB):
                        ins = nc.scalar.activation(rec[G % 2][:, k, 0:D], rec[G % 2][:, k, D:2 * D], ACT.Identity,
                                                   bias=rs2[:, 3, k:k + 1], scale=rs2[:, 1, k:k + 1])
                    ins.then_inc(a_xn2, 1)
                if j == 2 and is_group(g + 2):
                    H = g + 2
                    act.wait_ge(p_cT, per_group(H + 1, r))
                    if H >= 2:
                        act.wait_ge(p_v, per_group(H - 1, r))
                    nc.scalar.activation(cT[H % 2][:], X[:, 1, :], ACT.Copy).then_inc(a_cT, 1)
                if j == 3 and is_group(g + 2):
                    proj(1, g + 2, r)
                if is_batch(c - 2):
                    exps(c - 2, 1, r)
                if is_batch(c - 2):
                    exps(c - 2, 2, r)
                if j == 1 and is_group(g - 2):
                    G = g - 2
                    act.wait_ge(p_nT, per_group(G + 1, r))
                    nc.scalar.activation(xn2T[:], X[:, 0, :], ACT.Copy).then_inc(a_nT, 1)
                if j == 2 and is_group(g + 2):
                    H = g + 2
                    act.wait_ge(p_xT, per_group(H + 1, r))
                    if H >= 1:
                        act.wait_ge(p_q, per_group(H, r))
                    nc.scalar.activation(xnT[:], X[:, 0, :], ACT.Copy).then_inc(a_xT, 1)
                if j == 3 and is_group(g + 2):
                    proj(0, g + 2, r)
                if is_batch(c - 2):
                    exps(c - 2, 3, r)
                if is_batch(c - 4):
                    n = c - 4
                    act.wait_ge(p_oT, per_batch(n + 1, r))
                    if n >= 2:
                        act.wait_ge(p_at, per_batch(n - 1, r))
                    nc.scalar.activation(onT[n % 2][:], X[:, 1, 0:L], ACT.Copy).then_inc(a_oT, 1)
                if j == 2 and is_group(g - 2):
                    G = g - 2
                    act.wait_ge(v_ldif, per_group(G + 1, r))
                    nc.scalar.activation(lexp[:], ldif[:], ACT.Exp).then_inc(a_lexp, 1)

            act.wait_ge(s_bias, 64)
            nc.scalar.activation(tg[:], gains[:], ACT.Tanh).then_inc(s_tanh, 1)
            act.wait_ge(s_vset, 1)
            run_steps(step, act)

            def two(v, r, per=1):
                return v if r is None else r * (2 * per) + v

            def expert(e, r):
                p = e % 2
                act.wait_ge(p_eT, two(e + 1, r))
                if e >= 2:
                    act.wait_ge(p_H, two(4 * (e - 1), r, 4))
                nc.scalar.activation(xeT[p][:], S[:, p, :], ACT.Copy).then_inc(a_eT, 1)
                for f in (0, 2):
                    act.wait_ge(p_H, two(4 * e + f + 1, r, 4))
                    if e >= 2 and f == 0:
                        act.wait_ge(p_Y, two(e - 1, r))
                    nc.scalar.activation(hid[p][:, f, :], TS[:, f // 2, :], ACT.Relu, bias=b1_act[p][:, 0, f:f + 1]).then_inc(a_H, 1)
                if e < E - 1:
                    load_b1(e + 1, r)

            def load_b1(e, r):
                nc.scalar.activation(b1_act[e % 2][:], b1_all[:, bass.ds(two(e, r), 1), :], ACT.Copy)

            act.wait_ge(b12_in, 32)
            load_b1(0, None)

            expert(0, None)
            expert(1, None)
            with act.Fori(0, (E - 4) // 2) as r:
                for e in (2, 3):
                    expert(e, r)
            for e in (E - 2, E - 1):
                expert(e, None)

        @block.vector
        def _(dve):
            V = nc.vector

            def fence(i):
                return V.tensor_tensor(fence_v[:, i:i + 1], ident[:, 0:1], ident[:, 0:1], ALU.mult)

            def top(n, q, r):
                dve.wait_ge(p_S, per_batch(4 * n + q + 1, r, 4))
                if n >= 2 and q == 0:
                    dve.wait_ge(v_m, per_batch(n - 1, r))
                V.tensor_reduce(negm[n % 2][:, 4 * q:4 * q + 4], S[:, q % 2, :].rearrange("p (h k) -> p h k", h=4),
                                AX.X, ALU.max, negate=True).then_inc(v_red, 1)

            def split_max(n, r):
                dve.wait_ge(v_red, per_batch(4 * n + 4, r, 4))
                if n >= 2:
                    dve.wait_ge(p_m, per_batch(n - 1, r))
                V.tensor_copy(mpart[n % 2][:, 0, :], negm[n % 2][:]).then_inc(v_m1, 1)
                dve.wait_ge(v_m1, per_batch(n + 1, r))
                V.tensor_tensor(mpart[n % 2][:, 1, :], negm[n % 2][:], mpart[n % 2][:, 0, :], ALU.subtract).then_inc(v_m, 1)

            def normalise(n, r):
                o = X[:, 1, :].rearrange("p (h v) -> p h v", v=HV)
                dve.wait_ge(p_back, per_batch(n + 1, r))
                if n >= 1:
                    dve.wait_ge(v_on, per_batch(n, r))
                V.reciprocal(rl[:], o[:, :, HD]).then_inc(v_rl, 1)
                dve.wait_ge(v_rl, per_batch(n + 1, r))
                if n >= 2:
                    dve.wait_ge(p_oT, per_batch(n - 1, r))
                V.tensor_tensor(on[n % 2][:].rearrange("p (h d) -> p h d", d=HD), o[:, :, 0:HD],
                                rl[:].unsqueeze(2).broadcast_to([P, HEADS, HD]), ALU.mult).then_inc(v_on, 1)

            def residual(n, r):
                dve.wait_ge(p_at, per_batch(n + 1, r))
                dve.wait_ge(g_xb, per_group(n // GB + 1, r))
                G, row1 = n // GB, rec[n // GB % 2][:, n % GB, D:2 * D]
                if n % GB == 0:
                    dve.wait_ge(sent[G % 2], per_group(64 * (G // 2) + 16, r, 32))
                    if G >= 1:
                        dve.wait_ge(x1_out, per_group(16 * G, r, 16))
                row = x_sb[:, bass.ds(per_batch(n, r), 1), :].rearrange("p o d -> p (o d)")
                V.tensor_tensor(row1, X[:, 0, 0:D], row, ALU.add).then_inc(v_x1, 1)
                dve.wait_ge(v_x1, per_batch(n + 1, r))
                V.bn_stats(st2[:, n % GB, :], row1).then_inc(v_st2, 1)

            def moments2(G, r):
                dve.wait_ge(v_st2, per_batch(GB * G + GB, r))
                fence(1)
                for k in range(GB):
                    mm = V.bn_aggr(mv2[:, k, :], st2[:, k, :])
                mm.then_inc(v_mv2, 1)

            def moments1(H, r):
                if H >= 1:
                    dve.wait_ge(v_xn, per_group(H, r))
                else:
                    dve.wait_ge(x_in[0], 16)
                if H in (1, 2):
                    dve.wait_ge(x_in[H], 16)
                fence(2)
                for k in range(GB):
                    row = x_sb[:, bass.ds(per_group(H * GB + k, r, GB), 1), :].rearrange("p o d -> p (o d)")
                    mm = V.bn_stats(st1[:, k, :], row)
                mm.then_inc(v_st1, 1)
                dve.wait_ge(v_st1, per_group(H + 1, r))
                fence(2)
                for k in range(GB):
                    mm = V.bn_aggr(mv1[:, k, :], st1[:, k, :])
                mm.then_inc(v_mv1, 1)

            def normed1(H, r):
                dve.wait_ge(g_rs1, per_group(H + 1, r))
                if H >= 1:
                    dve.wait_ge(p_xT, per_group(H, r))
                for k in range(GB):
                    row = x_sb[:, bass.ds(per_group(H * GB + k, r, GB), 1), :].rearrange("p o d -> p (o d)")
                    mm = V.tensor_scalar(xn[:, k, :], row, rs1[:, 1, k:k + 1], rs1[:, 3, k:k + 1], ALU.mult, ALU.add)
                mm.then_inc(v_xn, 1)

            def value_rows(G, r):
                dve.wait_ge(p_v, per_group(G + 1, r))
                if G == 0:
                    dve.wait_ge(g_vals, 2)
                if G >= 2:
                    dve.wait_ge(p_O, per_batch(GB * (G - 2) + GB, r))
                V.tensor_tensor(vals[G % 2][:, :, :, 0:HD], X[:, 1, :].rearrange("p (k h d) -> p k h d", k=GB, d=HD),
                                bv[:].rearrange("p (h d) -> p h d", d=HD).unsqueeze(1).broadcast_to([P, GB, HEADS, HD]),
                                ALU.add).then_inc(v_v, 1)

            ROUTE = 6

            def route(G, r):
                def link(ins, i):
                    ins.then_inc(v_route, 1)
                    dve.wait_ge(v_route, per_group(ROUTE * G + i, r, ROUTE))

                dve.wait_ge(v_lg, per_group(G + 1, r))
                link(V.tensor_reduce(lmax[:], lgs[:], AX.X, ALU.max), 1)
                V.tensor_tensor(ldif[:], lgs[:], lmax[:].unsqueeze(2).broadcast_to([P, GB, E]), ALU.subtract).then_inc(v_ldif, 1)
                link(V.tensor_tensor(cand[:], lgs[:], lmax[:].unsqueeze(2).broadcast_to([P, GB, E]), ALU.is_lt), 2)
                link(V.scalar_tensor_tensor(cand[:], cand[:], float(E), iota, ALU.mult, ALU.add), 3)
                link(V.tensor_reduce(choice[:], cand[:], AX.X, ALU.min), 4)
                link(V.tensor_reduce(seen_g[:], mask[:].rearrange("p k e -> p e k"), AX.X, ALU.add), 5)
                link(V.tensor_tensor(seen[:], seen[:], seen_g[:], ALU.add), 6)
                V.tensor_tensor(mask[:], iota, choice[:].unsqueeze(2).broadcast_to([P, GB, E]), ALU.is_equal).then_inc(v_mask, 1)

            PLACE = 5

            def logits(G, r):
                dve.wait_ge(p_lg, per_group(G + 1, r))
                if G >= 1:
                    dve.wait_ge(v_slot, per_group(G, r))
                V.tensor_copy(lgs[:].rearrange("p k e -> p (k e)"), X[:, 1, 0:GB * E]).then_inc(v_lg, 1)

            def positions(G, r):
                dve.wait_ge(p_pos, per_group(G + 1, r))
                V.tensor_tensor(at_e[:].rearrange("p k e -> p (k e)"), X[:, 1, 0:GB * E],
                                mask[:].rearrange("p k e -> p (k e)"), ALU.mult).then_inc(v_pos, 1)

            def place(G, r):
                def link(ins, i):
                    ins.then_inc(v_place, 1)
                    dve.wait_ge(v_place, per_group(PLACE * G + i, r, PLACE))

                dve.wait_ge(v_pos, per_group(G + 1, r))
                dve.wait_ge(a_lexp, per_group(G + 1, r))
                V.tensor_reduce(lsum[:], lexp[:], AX.X, ALU.add)
                link(V.tensor_reduce(loc[:], at_e[:], AX.X, ALU.add), 1)
                V.tensor_scalar(over[:], loc[:], float(CAP), float(NONE), ALU.is_ge, ALU.mult)
                link(V.scalar_tensor_tensor(base[:], choice[:], float(CAP), loc[:], ALU.mult, ALU.add), 2)
                link(V.tensor_tensor(slot[G % 2][:], base[:], over[:], ALU.add), 3)
                link(V.reciprocal(rec[G % 2][:, :, 2 * D], lsum[:]), 4)
                link(V.tensor_copy(rec[G % 2][:, :, 2 * D + 1], token_code[:, bass.ds(per_group(G * GB, r, GB), GB)]), 5)
                fence(3).then_inc(v_slot, 1)

            def step(c, r):
                j, g = c % GB, c // GB
                if is_batch(c):
                    top(c, 0, r)
                if j == 0 and is_group(g):
                    value_rows(g, r)
                if is_batch(c):
                    top(c, 1, r)
                if is_batch(c - 4):
                    normalise(c - 4, r)
                if is_batch(c - 5):
                    residual(c - 5, r)
                if j == 0 and is_group(g - 2):
                    moments2(g - 2, r)
                if is_batch(c):
                    top(c, 2, r)
                if j == 0 and is_group(g + 2):
                    moments1(g + 2, r)
                if j == 2 and is_group(g - 2):
                    logits(g - 2, r)
                if j == 3 and is_group(g - 2):
                    positions(g - 2, r)
                if is_batch(c):
                    top(c, 3, r)
                    split_max(c, r)
                if j == 1 and is_group(g + 2):
                    normed1(g + 2, r)
                if j == 2 and is_group(g - 2):
                    route(g - 2, r)
                if j == 3 and is_group(g - 2):
                    place(g - 2, r)

            dve.wait_ge(s_cst, 16)
            V.tensor_copy(ident_b[:], ident)
            V.tensor_copy(before_b[:], cst[:, P:2 * P])
            V.memset(ones_b[:], 1.0)
            V.memset(mask[:], 0.0)
            V.memset(seen[:], 0.0)
            V.memset(ones_row[:], 1.0).then_inc(v_ones, 1)
            dve.wait_ge(s_wqkv, 16)
            dve.wait_ge(s_bias, 64)
            V.tensor_scalar(bq_s[:], bqk[:, 0:1], SCALE, None, ALU.mult)
            V.tensor_copy(wq_dh[:].rearrange("p (d h) -> p d h", h=HEADS), wqkv[:, 0:D].rearrange("p (h d) -> p d h", d=HD))
            V.tensor_copy(wk_dh[:].rearrange("p (d h) -> p d h", h=HEADS),
                          wqkv[:, D:2 * D].rearrange("p (h d) -> p d h", d=HD)).then_inc(s_vset, 1)

            for c in range(FIRST, LOOP0):
                if c == -4:
                    dve.wait_ge(s_late, 64)
                    dve.wait_ge(s_tanh, 1)
                    V.tensor_scalar(wout_g[:], wout[:], tg[:, 0:1], None, ALU.mult)
                    V.tensor_scalar(bout_g[:], bout[:], tg[:, 0:1], None, ALU.mult).then_inc(s_vset, 1)
                step(c, None)
            with dve.Fori(0, (LOOP1 - LOOP0) // BODY) as r:
                for c in range(LOOP0, LOOP0 + BODY):
                    step(c, r)
            for c in range(LOOP1, LAST + 1):
                step(c, None)

            def two(v, r, per=1):
                return v if r is None else r * (2 * per) + v

            def relus(e, r):
                p = e % 2
                for f in (1, 3):
                    dve.wait_ge(p_H, two(4 * e + f + 1, r, 4))
                    if e >= 2 and f == 1:
                        dve.wait_ge(p_Y, two(e - 1, r))
                    if f == 1 and e < E - 1:
                        if e >= 1:
                            dve.wait_ge(v_H, two(2 * e, r, 2))
                        load_b1(e + 1, r)
                    V.tensor_scalar(hid[p][:, f, :], O[:, f // 2, :], b1_dve[p][:, 0, f:f + 1], 0.0, ALU.add, ALU.max).then_inc(v_H, 1)

            def load_b1(e, r):
                return V.tensor_copy(b1_dve[e % 2][:], b1_all[:, bass.ds(two(e, r), 1), :])

            def finish(e, r):
                p = e % 2
                dve.wait_ge(xr_in[p], two(16 * (e // 2) + 16, r, 8))
                if e >= 2:
                    dve.wait_ge(fin_out[p], two(64 * (e // 2), r, 32))
                V.tensor_scalar(gate2[p][:], xr[p][:, :, D], tg[:, 1:2], None, ALU.mult).then_inc(v_gate2, 1)
                V.tensor_scalar(tok[p][:], xr[p][:, :, D + 1], -1.0, float(NONE), ALU.mult, ALU.add).then_inc(v_tok, 1)
                dve.wait_ge(p_Y, two(e + 1, r))
                if e >= 1:
                    dve.wait_ge(v_fin, two(e, r))
                V.tensor_tensor(yb[:].rearrange("p (t n) -> p t n", n=D), X[:, p, :].rearrange("p (t n) -> p t n", n=D),
                                b2_all[:, bass.ds(two(e, r), 1), :].broadcast_to([P, ET, D]), ALU.add).then_inc(v_yb, 1)
                dve.wait_ge(v_yb, two(e + 1, r))
                for t in range(ET):
                    mm = V.scalar_tensor_tensor(fin[p][:, t, :], yb[:, t * D:(t + 1) * D], gate2[p][:, t:t + 1],
                                                xr[p][:, t, 0:D], ALU.mult, ALU.add)
                mm.then_inc(v_fin, 1)

            dve.wait_ge(b12_in, 32)
            load_b1(0, None).then_inc(v_b1, 1)
            dve.wait_ge(v_b1, 1)
            relus(0, None)
            relus(1, None)
            finish(0, None)
            relus(2, None)
            finish(1, None)
            with dve.Fori(0, (E - 4) // 2) as r:
                for e in (3, 4):
                    relus(e, r)
                    finish(e - 1, r)
            relus(E - 1, None)
            finish(E - 2, None)
            finish(E - 1, None)

        @block.gpsimd
        def _(pool):
            G_ = nc.gpsimd

            def fence():
                return G_.tensor_tensor(fence_p[:], pool_c[:, 0, 0:1], pool_c[:, 0, 0:1], ALU.add).then_inc(g_fence, 1)

            def root(H, r, mv, rs, ready, e, done, used):
                pool.wait_ge(ready, per_group(H + 1, r))
                if H >= 1:
                    pool.wait_ge(used, per_group(H, r))
                G_.tensor_tensor(rs[:, 0, :], mv[:, :, 1], pool_c[:, 0, :], ALU.add)
                G_.tensor_tensor(rs[:, 2, :], pool_c[:, 2, :], mv[:, :, 0], ALU.subtract).then_inc(e, 1)
                pool.wait_ge(e, per_group(2 * H + 1, r, 2))
                G_.tensor_tensor(rs[:, 1, :], rs[:, 0, :], pool_c[:, 1, :], ALU.pow).then_inc(e, 1)
                pool.wait_ge(e, per_group(2 * H + 2, r, 2))
                G_.tensor_tensor(rs[:, 3, :], rs[:, 2, :], rs[:, 1, :], ALU.mult).then_inc(done, 1)

            def split(side, H, r):
                p, turn = H % 2, 2 * H + (0 if side == 1 else 1)
                pool.wait_ge((a_q, a_k)[side], per_group(H + 1, r))
                if H >= 1:
                    pool.wait_ge((g_q, g_k)[side], per_group(H, r))
                first = parts[side][p][:, 0, :]
                G_.tensor_tensor(rest[side][:], full[side][:], first, ALU.subtract)
                G_.tensor_tensor(parts[side][p][:, 1, :], full[side][:], first, ALU.subtract).then_inc(g_spl, 1)
                pool.wait_ge(g_spl, per_group(turn + 1, r, 2))
                G_.tensor_tensor(parts[side][p][:, 2, :], rest[side][:], parts[side][p][:, 1, :],
                                 ALU.subtract).then_inc((g_q, g_k)[side], 1)

            def scatter(G, r):
                p = G % 2
                if G == 0:
                    for q in sent:
                        pool.wait_ge(q, 16)
                pool.wait_ge(v_slot, per_group(G + 1, r))
                if G == NG - 1:
                    pool.wait_ge(g_fence, NG - 1)
                fence()
                for k in range(GB):
                    G_.indirect_dma_start(rec_dram, bass.IndirectOffsetOnAxis(slot[p][:, k:k + 1], 0), rec[p][:, k, :], None,
                                          bounds_check=T - 1, oob_is_err=False).then_inc(sent[p], 16)

            def step(c, r):
                j, g = c % GB, c // GB
                if j == 0 and is_group(g - 2):
                    root(g - 2, r, mv2, rs2, v_mv2, g_e2, g_rs2, a_xn2)
                if j == 0 and g - 3 == NG - 2:
                    scatter(NG - 2, None)
                if c == 0:
                    pool.wait_ge(s_zero, 1)
                    for i in range(2):
                        pool.dma_start(rec_dram[i * (T // 2):(i + 1) * (T // 2), :].rearrange("(p a) c -> p a c", p=P),
                                       zeros[:].unsqueeze(1).broadcast_to([P, T // P // 2, REC])).then_inc(sent[i], 16)
                if j == 0 and is_group(g + 1):
                    split(1, g + 1, r)
                if j == 0 and is_group(g + 2):
                    root(g + 2, r, mv1, rs1, v_mv1, g_e1, g_rs1, v_xn)
                if j == 1 and is_group(g + 1):
                    split(0, g + 1, r)
                if j == 2 and is_group(g + 1):
                    H = g + 1
                    pool.wait_ge(v_xn, per_group(H + 1, r))
                    if H <= 0:
                        pool.wait_ge(s_vset, 2)
                    rows = x_sb[:, bass.ds(per_group(H * GB, r, GB), GB), :]
                    G_.tensor_tensor(rows, rows, bout_g[:].unsqueeze(1).broadcast_to([P, GB, D]), ALU.add).then_inc(g_xb, 1)
                if j == 3 and is_group(g - 2) and g - 2 != NG - 2:
                    scatter(g - 2, r)

            G_.memset(pool_c[:, 0, :], EPS)
            G_.memset(pool_c[:, 1, :], -0.5)
            G_.memset(pool_c[:, 2, :], 0.0).then_inc(s_pset, 1)
            G_.memset(zeros[:], 0.0).then_inc(s_zero, 1)
            for i in range(2):
                G_.memset(vals[i][:, :, :, HD:HV], 0.0).then_inc(g_zero, 1)
            pool.wait_ge(g_zero, 2)
            for i in range(2):
                G_.memset(vals[i][:, :, :, HD:HD + 1], 1.0).then_inc(g_vals, 1)
            pool.wait_ge(s_pset, 1)
            run_steps(step, pool)

            def rows_out(e, r):
                p = e % 2
                pool.wait_ge(v_fin, e + 1 if r is None else r * 2 + (e + 1))
                pool.wait_ge(v_tok, e + 1 if r is None else r * 2 + (e + 1))
                pool.wait_ge(g_fence, r * 2 + (NG + e))
                fence()
                for t in range(ET):
                    G_.indirect_dma_start(out_rows, bass.IndirectOffsetOnAxis(tok[p][:, t:t + 1], 0), fin[p][:, t, :], None,
                                          bounds_check=T - 1, oob_is_err=False).then_inc(fin_out[p], 16)

            pool.wait_ge(x1_out, 16 * NG)
            with pool.Fori(0, E // 2) as r:
                for e in (0, 1):
                    rows_out(e, r)


_INS = ['x', 'ctx_1024', 'g_xattn', 'g_ffn', 'L0_xattn_W_qkv', 'L0_xattn_b_qkv', 'L0_xattn_W_out', 'L0_xattn_b_out',
        'L0_ffn_Wg', 'L0_ffn_W1', 'L0_ffn_b1', 'L0_ffn_W2', 'L0_ffn_b2']


def kernel(**inputs):
    import numpy as _np
    import concourse.bacc as _bacc
    from concourse import mybir as _mybir
    from concourse.bass_utils import run_bass_kernel_spmd as _run

    nc = _bacc.Bacc("TRN2", target_bir_lowering=False, num_devices=1)
    arrays, args = {}, []
    for name in _INS:
        a = _np.ascontiguousarray(inputs[name])
        arrays[f"in_{name}_dram"] = a
        args.append(nc.dram_tensor(f"in_{name}_dram", a.shape, _mybir.dt.from_np(a.dtype), kind="ExternalInput").ap())
    n_b, n_e, n_k = inputs['x'].shape[0], inputs['L0_ffn_Wg'].shape[1], GB
    tokens = _np.arange(n_b * P, dtype=_np.float32).reshape(n_b, P).T
    consts = _np.concatenate([_np.eye(P), _np.triu(_np.ones((P, P)), 1),
                              _np.tile(_np.arange(n_e), (P, n_k)), 2 * n_b * P - tokens], axis=1).astype(_np.float32)
    arrays["in_consts_dram"] = consts
    args.append(nc.dram_tensor("in_consts_dram", consts.shape, _mybir.dt.float32, kind="ExternalInput").ap())
    shape = tuple(inputs['x'].shape)
    args.append(nc.dram_tensor("out_0_dram", shape, _mybir.dt.float32, kind="ExternalOutput").ap())
    flamingo_kernel(nc, *args)
    r = _run(nc, [arrays], core_ids=[0])
    return r.results[0]["out_0_dram"]
```

```python
from contextlib import ExitStack

import concourse.bass as bass
from concourse import mybir

F32 = mybir.dt.float32
BF16 = mybir.dt.bfloat16
U32 = mybir.dt.uint32
ALU = mybir.AluOpType
ACT = mybir.ActivationFunctionType
AX = mybir.AxisListType

P = 128
GB = 4
BODY = 8
EPS = 1e-5
Q_PARTS = (0, 0, 0, 1, 1, 2)
K_PARTS = (0, 1, 2, 0, 1, 0)
REC = 2 * P + 2


def flamingo_kernel(nc, x, ctx_in, g_xattn, g_ffn, w_qkv, b_qkv, w_out, b_out, wg, w1, b1, w2, b2, consts, out):
    B, L, D = x.shape
    E, _, F = w1.shape
    T = B * L
    CAP = -(-T // E)
    HEADS = 16
    HD = D // HEADS
    HV = 32
    SCALE = float(HD) ** -0.5
    NG = B // GB
    GT = GB * L
    SLOTS = len(Q_PARTS)
    KR = SLOTS * HD
    KM = KR + 2
    FC = F // P
    ET = CAP // P
    NONE = 2 * T
    LOOP0, LOOP1 = BODY, B - BODY
    FIRST, LAST = -8, 4 * (NG - 1) + 11
    assert L == P and D == P and CAP == 4 * P and F == 4 * P and E == 8

    with ExitStack() as ctx:
        def sb(name, shape, dt=F32):
            return ctx.enter_context(nc.sbuf_tensor(name, shape, dt))

        def ps(name):
            return ctx.enter_context(nc.psum_tensor(name, [P, 2, 512], F32))

        def sem(name):
            return ctx.enter_context(nc.semaphore(name))

        def sem2(name):
            return [sem(name + "0"), sem(name + "1")]

        rec_dram = nc.dram_tensor("rec_dram", (T, REC), F32).ap()

        S = ps("S")
        TS = ps("TS")
        O = ps("O")
        X = ps("X")

        cst = sb("cst", [P, 2 * P + GB * E + B])
        ident = cst[:, 0:P]
        iota = cst[:, 2 * P:2 * P + GB * E].rearrange("p (k e) -> p k e", e=E)
        token_code = cst[:, 2 * P + GB * E:]
        ident_b = sb("ident_b", [P, P], BF16)
        before_b = sb("before_b", [P, P], BF16)
        ones_b = sb("ones_b", [P, P], BF16)
        wqkv = sb("wqkv", [P, 3 * D])
        wq_dh = sb("wq_dh", [P, D])
        wk_dh = sb("wk_dh", [P, D])
        bqk = sb("bqk", [P, 2])
        bq_s = sb("bq_s", [P, 1])
        bv = sb("bv", [P, D])
        wout = sb("wout", [P, D])
        wout_g = sb("wout_g", [P, D])
        bout = sb("bout", [P, D])
        bout_g = sb("bout_g", [P, D])
        wg_sb = sb("wg_sb", [P, E])
        gains = sb("gains", [P, 2])
        tg = sb("tg", [P, 2])
        pool_c = sb("pool_c", [P, 2, GB])
        zeros = sb("zeros", [P, REC])
        fence_v = sb("fence_v", [P, 5])
        fence_p = sb("fence_p", [P, 1])

        x_sb = sb("x_sb", [P, B, D])
        c_sb = [sb(f"c_sb{i}", [P, GB, D]) for i in range(2)]
        cT = [sb(f"cT{i}", [P, GT]) for i in range(2)]
        xn = sb("xn", [P, GB, D])
        xnT = sb("xnT", [P, GT])
        st1 = sb("st1", [P, GB, 6])
        mv1 = sb("mv1", [P, GB, 2])
        rs1 = sb("rs1", [P, 2, GB])
        full = [sb(f"full_{s}", [P, GT]) for s in "qk"]
        rest = [sb(f"rest_{s}", [P, GT]) for s in "qk"]
        parts = [[sb(f"parts_{s}{i}", [P, 3, GT], BF16) for i in range(2)] for s in "qk"]
        qp = [sb(f"qp{i}", [P, HEADS, GT], BF16) for i in range(2)]
        kp = [sb(f"kp{i}", [P, HEADS, GT], BF16) for i in range(2)]
        vals = [sb(f"vals{i}", [P, GB, HEADS, HV]) for i in range(2)]
        ones_row = sb("ones_row", [2 * HEADS, GT], BF16)
        oraw = [sb(f"oraw{i}", [P, 4 * L]) for i in range(2)]
        negm = [sb(f"negm{i}", [P, HEADS]) for i in range(2)]
        mpart = [sb(f"mpart{i}", [P, 2, HEADS], BF16) for i in range(2)]
        mrow = [sb(f"mrow{i}", [2 * HEADS, P], BF16) for i in range(2)]
        prob = [sb(f"prob{i}", [P, HEADS * L]) for i in range(2)]
        rl = sb("rl", [P, HEADS])
        on = [sb(f"on{i}", [P, D]) for i in range(2)]
        onT = [sb(f"onT{i}", [P, L]) for i in range(2)]
        st2 = sb("st2", [P, GB, 6])
        mv2 = sb("mv2", [P, GB, 2])
        rs2 = sb("rs2", [P, 2, GB])
        rec = [sb(f"rec{i}", [P, GB, REC]) for i in range(2)]
        xn2T = sb("xn2T", [P, GT])
        lgs = sb("lgs", [P, GB, E])
        lmax = sb("lmax", [P, GB])
        ldif = sb("ldif", [P, GB, E])
        lexp = sb("lexp", [P, GB, E])
        lsum = sb("lsum", [P, GB])
        cand = sb("cand", [P, GB, E])
        choice = sb("choice", [P, GB])
        mask = sb("mask", [P, GB, E], BF16)
        seen = sb("seen", [P, E], BF16)
        seen_g = sb("seen_g", [P, E])
        at_e = sb("at_e", [P, GB, E])
        loc = sb("loc", [P, GB])
        over = sb("over", [P, GB])
        base = sb("base", [P, GB])
        slot = [sb(f"slot{i}", [P, GB], U32) for i in range(2)]
        w1s = [sb(f"w1s{i}", [P, F]) for i in range(2)]
        w2s = [sb(f"w2s{i}", [P, FC, D]) for i in range(2)]
        b1_all = sb("b1_all", [P, E, FC])
        b2_all = sb("b2_all", [P, E, D])
        b1_act = [sb(f"b1_act{i}", [P, 1, FC]) for i in range(2)]
        b1_dve = [sb(f"b1_dve{i}", [P, 1, FC]) for i in range(2)]
        xe = [sb(f"xe{i}", [P, ET, D]) for i in range(2)]
        xr = [sb(f"xr{i}", [P, ET, REC - D]) for i in range(2)]
        xeT = [sb(f"xeT{i}", [P, CAP]) for i in range(2)]
        hid = [qp[i][:, 0:8, :].rearrange("p h n -> p (h n)").bitcast(F32).rearrange("p (f n) -> p f n", f=FC)
               for i in range(2)]
        yb = sb("yb", [P, CAP])
        gate2 = [sb(f"gate2_{i}", [P, ET]) for i in range(2)]
        tok = [sb(f"tok{i}", [P, ET], U32) for i in range(2)]
        fin = [sb(f"fin{i}", [P, ET, D]) for i in range(2)]

        s_cst, s_wqkv, s_bias, s_late = sem("s_cst"), sem("s_wqkv"), sem("s_bias"), sem("s_late")
        s_zero, s_vset, s_tanh, s_pset = sem("s_zero"), sem("s_vset"), sem("s_tanh"), sem("s_pset")
        x_in = [sem(f"x_in{i}") for i in range(3)]
        c_in, q_in, k_in, m_in = sem2("c_in"), sem2("q_in"), sem2("k_in"), sem2("m_in")
        x1_out, sent = sem("x1_out"), sem2("sent")
        p_cT, p_xT, p_q, p_k, p_v = sem("p_cT"), sem("p_xT"), sem("p_q"), sem("p_k"), sem("p_v")
        g_zero = sem("g_zero")
        v_ones, g_vals = sem("v_ones"), sem("g_vals")
        p_back, a_O, s_ones = sem("p_back"), sem("a_O"), sem("s_ones")
        p_S, p_m, p_T, p_O, p_oT, p_at = sem("p_S"), sem("p_m"), sem("p_T"), sem("p_O"), sem("p_oT"), sem("p_at")
        p_nT, p_lg, p_pos = sem("p_nT"), sem("p_lg"), sem("p_pos")
        a_cT, a_xT, a_q, a_k, a_m = sem("a_cT"), sem("a_xT"), sem("a_q"), sem("a_k"), sem("a_m")
        a_exp, a_oT, a_nT, a_lexp = sem("a_exp"), sem("a_oT"), sem("a_nT"), sem("a_lexp")
        v_st1, v_mv1, v_xn, v_v, v_red, v_m1, v_m = (sem("v_st1"), sem("v_mv1"), sem("v_xn"), sem("v_v"), sem("v_red"),
                                                     sem("v_m1"), sem("v_m"))
        v_rl, v_on, v_x1, v_st2, v_mv2, g_xn2 = sem("v_rl"), sem("v_on"), sem("v_x1"), sem("v_st2"), sem("v_mv2"), sem("g_xn2")
        v_lg, v_ldif, v_route, v_mask, v_pos, v_place, v_slot = (sem("v_lg"), sem("v_ldif"), sem("v_route"), sem("v_mask"),
                                                                sem("v_pos"), sem("v_place"), sem("v_slot"))
        g_e1, g_rs1, g_e2, g_rs2, g_xb, q_split, k_split = (sem("g_e1"), sem("g_rs1"), sem("g_e2"), sem("g_rs2"), sem("g_xb"),
                                                           sem("q_split"), sem("k_split"))
        g_fence, a_qf, a_kf = sem("g_fence"), sem("a_qf"), sem("a_kf")
        q_rest, k_rest = sem("q_rest"), sem("k_rest")
        w1_in, w2_in, xe_in, xr_in, fin_out = sem2("w1_in"), sem2("w2_in"), sem2("xe_in"), sem2("xr_in"), sem2("fin_out")
        b12_in, v_b1 = sem("b12_in"), sem("v_b1")
        p_eT, p_H, p_Y = sem("p_eT"), sem("p_H"), sem("p_Y")
        a_eT, a_H, v_H, v_yb, v_gate2, v_tok, v_fin = (sem("a_eT"), sem("a_H"), sem("v_H"), sem("v_yb"), sem("v_gate2"),
                                                       sem("v_tok"), sem("v_fin"))

        x_v = x.rearrange("b p d -> p b d")
        out_v = out.rearrange("b p d -> p b d")
        out_rows = out.rearrange("b p d -> (b p) d")
        ctx_v = ctx_in.rearrange("b p d -> p b d")
        rec_v = rec_dram.rearrange("(e t p) c -> e p t c", t=ET, p=P)

        def per_batch(v, r, per=1):
            return v if r is None else r * (per * BODY) + v

        def per_group(v, r, per=1):
            return v if r is None else r * (per * BODY // GB) + v

        def is_batch(n):
            return 0 <= n < B

        def is_group(g):
            return 0 <= g < NG

        BATCH_TASKS = ("m", "at", "back", "oT")

        def x_tasks(c):
            j, g = c % GB, c // GB
            first = {1: ("v", g), 2: ("cT", g + 2), 3: ("k", g + 2)}.get(j)
            third = {2: ("lg", g - 2), 3: ("pos", g - 2)}.get(j)
            if g + 2 == 0:
                first, third = (first, ("k", 0)) if j == 2 else (None if j == 3 else first, third)
            second = {1: ("nT", g - 2), 2: ("xT", g + 2), 3: ("q", g + 2)}.get(j)
            bank0 = [("at", c - 5), ("m", c - 1), second]
            bank1 = [first, ("back", c - 4), third, ("oT", c - 4)]
            ok = lambda t: t is not None and (is_batch(t[1]) if t[0] in BATCH_TASKS else is_group(t[1]))
            return [[t for t in bank0 if ok(t)], [t for t in bank1 if ok(t)]]

        before = {}
        for bank in range(2):
            last = None
            for c in range(FIRST, LAST + 1):
                for t in x_tasks(c)[bank]:
                    before[t] = last
                    last = t
        emptied = {"v": v_v, "cT": a_cT, "k": a_kf, "lg": v_lg, "pos": v_pos, "nT": a_nT, "xT": a_xT, "q": a_qf,
                   "m": a_m, "at": v_x1, "back": v_on, "oT": a_oT}

        def bank_free(eng, name, idx, r):
            t = before[(name, idx)]
            if t is not None:
                step = per_batch if t[0] in BATCH_TASKS else per_group
                eng.wait_ge(emptied[t[0]], step(t[1] + 1, r))

        def split(eng, ops, side, H, r):
            p = H % 2
            eng.wait_ge((a_q, a_k)[side], per_group(H + 1, r))
            if H >= 1:
                eng.wait_ge((q_split, k_split)[side], per_group(H, r))
            first = parts[side][p][:, 0, :]
            ops.tensor_tensor(rest[side][:], full[side][:], first, ALU.subtract)
            ops.tensor_tensor(parts[side][p][:, 1, :], full[side][:], first, ALU.subtract).then_inc((q_rest, k_rest)[side], 1)
            eng.wait_ge((q_rest, k_rest)[side], per_group(H + 1, r))
            ops.tensor_tensor(parts[side][p][:, 2, :], rest[side][:], parts[side][p][:, 1, :],
                              ALU.subtract).then_inc((q_split, k_split)[side], 1)

        def run_steps(step_fn, eng):
            for c in range(FIRST, LOOP0):
                step_fn(c, None)
            with eng.Fori(0, (LOOP1 - LOOP0) // BODY) as r:
                for c in range(LOOP0, LOOP0 + BODY):
                    step_fn(c, r)
            for c in range(LOOP1, LAST + 1):
                step_fn(c, None)

        block = ctx.enter_context(nc.Block())

        @block.sync
        def _(sp):
            sp.dma_start(x_sb[:, 0:GB, :], x_v[:, 0:GB, :]).then_inc(x_in[0], 16)
            sp.dma_start(cst[:], consts).then_inc(s_cst, 16)
            sp.dma_start(wqkv[:], w_qkv).then_inc(s_wqkv, 16)
            for i in range(2):
                sp.dma_start(bqk[:, i:i + 1], b_qkv[i * D:(i + 1) * D].rearrange("(h d o) -> d h o", d=HD, o=1),
                             allow_slow_non_contiguous=True).then_inc(s_bias, 16)
            sp.dma_start(gains[:, 0:1], g_xattn.rearrange("(a n) -> a n", a=1).broadcast_to([P, 1])).then_inc(s_bias, 16)
            sp.dma_start(gains[:, 1:2], g_ffn.rearrange("(a n) -> a n", a=1).broadcast_to([P, 1])).then_inc(s_bias, 16)

            def moved(view, offset):
                return view if offset is None else bass.AP(view.tensor, offset, view.ap)

            def load_w1(e, at):
                sp.dma_start(w1s[e % 2][:], moved(w1[e % 2], at)).then_inc(w1_in[e % 2], 16)

            def load_w2(e, at):
                sp.dma_start(w2s[e % 2][:], moved(w2[e % 2].rearrange("(f p) n -> p f n", p=P), at)).then_inc(w2_in[e % 2], 16)

            scratch = sp.alloc_register("ready")

            def ready(*values):
                for v in values:
                    if not isinstance(v, int):
                        sp.reg_mov(scratch, v)

            def late_loads():
                sp.dma_start(x_sb[:, GB:2 * GB, :], x_v[:, GB:2 * GB, :]).then_inc(x_in[1], 16)
                sp.dma_start(bv[:], b_qkv[2 * D:3 * D].rearrange("(a n) -> a n", a=1).broadcast_to([P, D])).then_inc(s_late, 16)
                sp.dma_start(bout[:], b_out.rearrange("(a n) -> a n", a=1).broadcast_to([P, D])).then_inc(s_late, 16)
                sp.dma_start(wout[:], w_out).then_inc(s_late, 16)
                sp.dma_start(wg_sb[:], wg).then_inc(s_late, 16)

            pieces = [("k", s) for s in range(SLOTS)] + [("q", s) for s in range(SLOTS)]

            def pack(H, r, lo, hi):
                p = H % 2
                if lo == 0:
                    ready(per_batch(4 * (GB * H - 5) + 4, r, 4), per_group(H + 1, r))
                    if H >= 2:
                        sp.wait_ge(p_T, per_batch(4 * (GB * H - 5) + 4, r, 4))
                    sp.wait_ge(k_split, per_group(H + 1, r))
                    sp.wait_ge(a_k, per_group(H + 1, r))
                for side, s in pieces[lo:hi]:
                    if (side, s) == ("q", 0):
                        sp.wait_ge(q_split, per_group(H + 1, r))
                        sp.wait_ge(a_q, per_group(H + 1, r))
                    dst = (kp if side == "k" else qp)[p][s * HD:(s + 1) * HD, :, :]
                    src = parts[side == "k"][p][:, (K_PARTS if side == "k" else Q_PARTS)[s], :]
                    sp.dma_start(dst, src).then_inc((k_in if side == "k" else q_in)[p], 16)

            def step(c, r):
                j, g = c % GB, c // GB
                if j == 2 and is_group(g + 1):
                    pack(g + 1, r, 0, SLOTS)
                loads, stores = j == 0 and is_group(g + 2), j == 0 and is_group(g - 2)
                if j == 0:
                    ready(per_batch(c, r), per_group(g + 1, r), per_batch(GB * (g - 2) + GB, r))
                if is_batch(c - 1):
                    sp.wait_ge(a_m, per_batch(c, r))
                if is_batch(c - 1):
                    n, p = c - 1, (c - 1) % 2
                    G = n // GB
                    t0 = (n % GB) * L
                    sp.dma_start(qp[G % 2][KR:KM, :, t0:t0 + L], mrow[p][:]).then_inc(m_in[p], 16)
                if stores:
                    sp.wait_ge(v_x1, per_batch(GB * (g - 2) + GB, r))
                    sl = bass.ds(per_group((g - 2) * GB, r, GB), GB)
                    sp.dma_start(out_v[:, sl, :], rec[g % 2][:, :, D:2 * D]).then_inc(x1_out, 16)
                if loads:
                    if g + 2 >= 2:
                        sp.wait_ge(p_cT, per_group(g + 1, r))
                    sp.dma_start(c_sb[g % 2][:], ctx_v[:, bass.ds(per_group((g + 2) * GB, r, GB), GB), :]).then_inc(c_in[g % 2], 16)
                if j == 2 and is_group(g + 1):
                    pack(g + 1, r, SLOTS, 2 * SLOTS)
                if c == -8:
                    late_loads()
                if c == -7:
                    sp.dma_start(x_sb[:, 2 * GB:, :], x_v[:, 2 * GB:, :]).then_inc(x_in[2], 16)
                if c == -1:
                    sp.wait_ge(v_ones, 1)
                    for i in range(2):
                        sp.dma_start(kp[i][KR:KM, :, :], ones_row[:]).then_inc(s_ones, 16)
                if c == B + 2:
                    for e in range(2):
                        load_w1(e, None)
                        load_w2(e, None)
                    sp.dma_start(b1_all[:], b1.rearrange("e (f p) -> p e f", p=P),
                                 allow_slow_non_contiguous=True).then_inc(b12_in, 16)
                    sp.dma_start(b2_all[:], b2.rearrange("(a e) n -> a (e n)", a=1).broadcast_to([P, E * D])).then_inc(b12_in, 16)

            run_steps(step, sp)

            def load_xe(e, at):
                sp.dma_start(xe[e % 2][:], moved(rec_v[e % 2][:, :, 0:D], at)).then_inc(xe_in[e % 2], 16)

            def load_xr(e, at):
                sp.dma_start(xr[e % 2][:], moved(rec_v[e % 2][:, :, D:REC], at)).then_inc(xr_in[e % 2], 16)

            for p in range(2):
                sp.wait_ge(sent[p], 64 + 16 * GB * (NG // 2))
            for e in range(2):
                load_xe(e, None)
            for e in range(2):
                load_xr(e, None)
            sp.wait_ge(p_eT, 1)
            load_xe(2, 2 * CAP * REC)

            def loads(e, r):
                def at(v, per):
                    return v if r is None else r * (2 * per) + v

                w_at = at(e * D * F, D * F)
                xe_at, xr_at = at((e + 1) * CAP * REC, CAP * REC), at(e * CAP * REC + D, CAP * REC)
                turned, used, through = at(e, 1), at(4 * (e - 1), 4), at(e - 1, 1)
                ready(w_at * 4, xe_at * 4, xr_at * 4, turned, used, through)
                sp.wait_ge(p_H, used)
                load_w1(e, w_at)
                if e < E - 1:
                    sp.wait_ge(p_eT, turned)
                    load_xe(e + 1, xe_at)
                sp.wait_ge(p_Y, through)
                load_w2(e, w_at)
                sp.wait_ge(v_fin, through)
                load_xr(e, xr_at)

            with sp.Fori(0, (E - 4) // 2) as r:
                for e in (2, 3):
                    loads(e, r)
            for e in (E - 2, E - 1):
                loads(e, None)
            sp.wait_ge(x1_out, 16 * NG)
            for p in range(2):
                sp.wait_ge(fin_out[p], 16 * ET * (E // 2))

        @block.tensor
        def _(pe):
            def group_task(name, idx, r):
                bank_free(pe, name, idx, r)
                if name == "cT":
                    pe.wait_ge(c_in[idx % 2], per_group(16 * (idx // 2) + 16, r, 8))
                    if idx == 0:
                        pe.wait_ge(s_cst, 16)
                    for k in range(GB):
                        mm = nc.tensor.transpose(X[:, 1, k * L:(k + 1) * L], c_sb[idx % 2][:, k, :], ident)
                    mm.then_inc(p_cT, 1)
                elif name == "xT":
                    pe.wait_ge(v_xn, per_group(idx + 1, r))
                    for k in range(GB):
                        mm = nc.tensor.transpose(X[:, 0, k * L:(k + 1) * L], xn[:, k, :], ident)
                    mm.then_inc(p_xT, 1)
                elif name == "k":
                    pe.wait_ge(a_cT, per_group(idx + 1, r))
                    if idx == 0:
                        pe.wait_ge(s_vset, 1)
                    nc.tensor.matmul(X[:, 1, :], wk_dh[:], cT[idx % 2][:], start=True, stop=True).then_inc(p_k, 1)
                elif name == "q":
                    pe.wait_ge(a_xT, per_group(idx + 1, r))
                    nc.tensor.matmul(X[:, 0, :], wq_dh[:], xnT[:], start=True, stop=True).then_inc(p_q, 1)
                elif name == "v":
                    for k in range(GB):
                        mm = nc.tensor.matmul(X[:, 1, k * L:(k + 1) * L], cT[idx % 2][:, k * L:(k + 1) * L],
                                              wqkv[:, 2 * D:3 * D], start=True, stop=True)
                    mm.then_inc(p_v, 1)
                elif name == "nT":
                    pe.wait_ge(g_xn2, per_group(idx + 1, r))
                    for k in range(GB):
                        mm = nc.tensor.transpose(X[:, 0, k * L:(k + 1) * L], rec[idx % 2][:, k, 0:D], ident)
                    mm.then_inc(p_nT, 1)
                elif name == "lg":
                    pe.wait_ge(a_nT, per_group(idx + 1, r))
                    for k in range(GB):
                        mm = nc.tensor.matmul(X[:, 1, k * E:(k + 1) * E], xn2T[:, k * L:(k + 1) * L], wg_sb[:],
                                              start=True, stop=True)
                    mm.then_inc(p_lg, 1)
                elif name == "pos":
                    pe.wait_ge(v_mask, per_group(idx + 1, r))
                    for k in range(GB):
                        o = X[:, 1, k * E:(k + 1) * E]
                        nc.tensor.matmul(o, before_b[:], mask[:, k, :], start=True, stop=False)
                        for k2 in range(k):
                            nc.tensor.matmul(o, ones_b[:], mask[:, k2, :], start=False, stop=False)
                        mm = nc.tensor.matmul(o, ones_b[:], seen[:], start=False, stop=True)
                    mm.then_inc(p_pos, 1)

            def scores(n, q, r):
                G, t0 = n // GB, (n % GB) * L
                if q == 0 and n % GB == 0:
                    pe.wait_ge(q_in[G % 2], per_group(96 * (G // 2) + 96, r, 48))
                    pe.wait_ge(k_in[G % 2], per_group(96 * (G // 2) + 96, r, 48))
                if 4 * n + q >= 2:
                    pe.wait_ge(v_red, per_batch(4 * n + q - 1, r, 4))
                for h in range(4 * q, 4 * q + 4):
                    o = (h % 4) * L
                    mm = nc.tensor.matmul(S[:, q % 2, o:o + L], qp[G % 2][0:KR, h, t0:t0 + L],
                                          kp[G % 2][0:KR, h, t0:t0 + L], start=True, stop=True)
                mm.then_inc(p_S, 1)

            def shifted(n, q, r):
                G, t0 = n // GB, (n % GB) * L
                if q == 0:
                    if n == 0:
                        pe.wait_ge(s_ones, 32)
                    pe.wait_ge(m_in[n % 2], per_batch(16 * (n // 2) + 16, r, 8))
                if 4 * n + q >= 2:
                    pe.wait_ge(a_exp, per_batch(4 * n + q - 1, r, 4))
                for h in range(4 * q, 4 * q + 4):
                    o = (h % 4) * L
                    mm = nc.tensor.matmul(TS[:, q % 2, o:o + L], kp[G % 2][0:KM, h, t0:t0 + L],
                                          qp[G % 2][0:KM, h, t0:t0 + L], start=True, stop=True)
                mm.then_inc(p_T, 1)

            def values(n, q, r):
                G, k = n // GB, n % GB
                pe.wait_ge(a_exp, per_batch(4 * n + q + 1, r, 4))
                if q == 0:
                    if k == 0:
                        pe.wait_ge(v_v, per_group(G + 1, r))
                    if n >= 2:
                        pe.wait_ge(a_O, per_batch(n - 1, r))
                for h in range(4 * q, 4 * q + 4):
                    i = h % 4
                    mm = nc.tensor.matmul(O[i * HV:(i + 1) * HV, n % 2, q * L:(q + 1) * L], vals[G % 2][:, k, h, :],
                                          prob[n % 2][:, h * L:(h + 1) * L], start=True, stop=True)
                if q == 3:
                    mm.then_inc(p_O, 1)

            def step(c, r):
                todo = x_tasks(c)[::-1 if c < 0 else 1]
                groups = [t for bank in todo for t in bank if t[0] not in BATCH_TASKS]
                j = c % GB
                at_q = {0: [t for t in groups if t[0] in ("v", "cT") or t[0] == "k" and j == 3], 1: [],
                        2: [t for t in groups if t[0] in ("lg", "pos", "xT", "q") or t[0] == "k" and j == 2],
                        3: [t for t in groups if t[0] == "nT"]}
                for q in range(4):
                    if is_batch(c):
                        scores(c, q, r)
                    if is_batch(c - 2):
                        shifted(c - 2, q, r)
                    for t in at_q[q]:
                        group_task(t[0], t[1], r)
                    if q == 0 and is_batch(c - 5):
                        bank_free(pe, "at", c - 5, r)
                        pe.wait_ge(a_oT, per_batch(c - 4, r))
                        nc.tensor.matmul(X[:, 0, 0:D], onT[(c - 5) % 2][:], wout_g[:], start=True, stop=True).then_inc(p_at, 1)
                    if q == 1 and is_batch(c - 4):
                        bank_free(pe, "back", c - 4, r)
                        pe.wait_ge(a_O, per_batch(c - 3, r))
                        for i in range(4):
                            mm = nc.tensor.transpose(X[:, 1, i * L:(i + 1) * L], oraw[c % 2][:, i * L:(i + 1) * L], ident)
                        mm.then_inc(p_back, 1)
                    if q == 1 and is_batch(c - 1):
                        bank_free(pe, "m", c - 1, r)
                        pe.wait_ge(v_m, per_batch(c, r))
                        nc.tensor.transpose(X[:, 0, 0:P // 2].bitcast(BF16)[0:2 * HEADS, :],
                                            mpart[(c - 1) % 2][:].rearrange("p j h -> p (j h)"), ident_b[:]).then_inc(p_m, 1)
                    if q == 3 and is_batch(c - 4):
                        bank_free(pe, "oT", c - 4, r)
                        pe.wait_ge(v_on, per_batch(c - 3, r))
                        nc.tensor.transpose(X[:, 1, 0:L], on[c % 2][:], ident).then_inc(p_oT, 1)
                    if is_batch(c - 3):
                        values(c - 3, q, r)

            run_steps(step, pe)

            def two(v, r, per=1):
                return v if r is None else r * (2 * per) + v

            def turn(e, r):
                pe.wait_ge(xe_in[e % 2], two(16 * (e // 2) + 16, r, 8))
                if e >= 2:
                    pe.wait_ge(a_eT, two(e - 1, r))
                for t in range(ET):
                    mm = nc.tensor.transpose(S[:, e % 2, t * P:(t + 1) * P], xe[e % 2][:, t, 0:D], ident)
                mm.then_inc(p_eT, 1)

            def hidden(e, r):
                pe.wait_ge(a_eT, two(e + 1, r))
                pe.wait_ge(w1_in[e % 2], two(16 * (e // 2) + 16, r, 8))
                for f in range(FC):
                    if e >= 1:
                        pe.wait_ge(a_H if f % 2 == 0 else v_H, two(2 * (e - 1) + f // 2 + 1, r, 2))
                    bank = (TS if f % 2 == 0 else O)[:, f // 2, :]
                    nc.tensor.matmul(bank, w1s[e % 2][:, f * P:(f + 1) * P], xeT[e % 2][:], start=True, stop=True).then_inc(p_H, 1)

            def outputs(e, r):
                pe.wait_ge(a_H, two(2 * e + 2, r, 2))
                pe.wait_ge(v_H, two(2 * e + 2, r, 2))
                pe.wait_ge(w2_in[e % 2], two(16 * (e // 2) + 16, r, 8))
                if e >= 2:
                    pe.wait_ge(v_yb, two(e - 1, r))
                for t in range(ET):
                    for f in range(FC):
                        mm = nc.tensor.matmul(X[:, e % 2, t * P:(t + 1) * P], hid[e % 2][:, f, t * P:(t + 1) * P],
                                              w2s[e % 2][:, f, :], start=(f == 0), stop=(f == FC - 1))
                mm.then_inc(p_Y, 1)

            turn(0, None)
            hidden(0, None)
            turn(1, None)
            hidden(1, None)
            turn(2, None)
            outputs(0, None)
            hidden(2, None)
            with pe.Fori(0, (E - 4) // 2) as r:
                for e in (3, 4):
                    turn(e, r)
                    outputs(e - 2, r)
                    hidden(e, r)
            turn(E - 1, None)
            outputs(E - 3, None)
            hidden(E - 1, None)
            outputs(E - 2, None)
            outputs(E - 1, None)

        @block.scalar
        def _(act):
            def proj(side, H, r):
                act.wait_ge((p_q, p_k)[side], per_group(H + 1, r))
                if H >= 1:
                    act.wait_ge((q_split, k_split)[side], per_group(H, r))
                bias = bq_s[:, 0:1] if side == 0 else bqk[:, 1:2]
                nc.scalar.activation(full[side][:], X[:, side, :], ACT.Identity, bias=bias,
                                     scale=(SCALE, 1.0)[side]).then_inc((a_qf, a_kf)[side], 1)

            def first_part(side, H, r):
                act.wait_ge((a_qf, a_kf)[side], per_group(H + 1, r))
                if H >= 2:
                    act.wait_ge((q_in, k_in)[side][H % 2], per_group(96 * (H // 2), r, 48))
                nc.scalar.activation(parts[side][H % 2][:, 0, :], full[side][:], ACT.Copy).then_inc((a_q, a_k)[side], 1)

            def exps(n, q, r):
                act.wait_ge(p_T, per_batch(4 * n + q + 1, r, 4))
                if n >= 2:
                    if q == 0:
                        act.wait_ge(p_O, per_batch(n - 1, r))
                nc.scalar.activation(prob[n % 2][:, q * 512:(q + 1) * 512], TS[:, q % 2, :], ACT.Exp).then_inc(a_exp, 1)

            def step(c, r):
                j, g = c % GB, c // GB
                if is_batch(c - 4):
                    n = c - 4
                    act.wait_ge(p_O, per_batch(n + 1, r))
                    if n >= 2:
                        act.wait_ge(p_back, per_batch(n - 1, r))
                    nc.scalar.activation(oraw[n % 2][:], O[:, n % 2, :], ACT.Copy).then_inc(a_O, 1)
                if is_batch(c - 2):
                    exps(c - 2, 0, r)
                if j == 2 and is_group(g + 2):
                    H = g + 2
                    act.wait_ge(p_cT, per_group(H + 1, r))
                    if H >= 2:
                        act.wait_ge(p_v, per_group(H - 1, r))
                    nc.scalar.activation(cT[H % 2][:], X[:, 1, :], ACT.Copy).then_inc(a_cT, 1)
                if j == (3 if g + 2 else 2) and is_group(g + 2):
                    proj(1, g + 2, r)
                if is_batch(c - 1):
                    n = c - 1
                    act.wait_ge(p_m, per_batch(n + 1, r))
                    if n >= 2:
                        act.wait_ge(m_in[n % 2], per_batch(16 * (n // 2), r, 8))
                    nc.scalar.activation(mrow[n % 2][:], X[:, 0, 0:P // 2].bitcast(BF16)[0:2 * HEADS, :],
                                         ACT.Copy).then_inc(a_m, 1)
                if is_batch(c - 2):
                    exps(c - 2, 1, r)
                if j == (3 if g + 2 else 2) and is_group(g + 2):
                    first_part(1, g + 2, r)
                if is_batch(c - 2):
                    exps(c - 2, 2, r)
                if j == 2 and is_group(g + 2):
                    H = g + 2
                    act.wait_ge(p_xT, per_group(H + 1, r))
                    if H >= 1:
                        act.wait_ge(p_q, per_group(H, r))
                    nc.scalar.activation(xnT[:], X[:, 0, :], ACT.Copy).then_inc(a_xT, 1)
                if j == 3 and is_group(g + 2):
                    proj(0, g + 2, r)
                if is_batch(c - 2):
                    exps(c - 2, 3, r)
                if j == 1 and is_group(g - 2):
                    G = g - 2
                    act.wait_ge(p_nT, per_group(G + 1, r))
                    nc.scalar.activation(xn2T[:], X[:, 0, :], ACT.Copy).then_inc(a_nT, 1)
                if is_batch(c - 4):
                    n = c - 4
                    act.wait_ge(p_oT, per_batch(n + 1, r))
                    if n >= 2:
                        act.wait_ge(p_at, per_batch(n - 1, r))
                    nc.scalar.activation(onT[n % 2][:], X[:, 1, 0:L], ACT.Copy).then_inc(a_oT, 1)
                if j == 3 and is_group(g + 2):
                    first_part(0, g + 2, r)
                if j == 2 and is_group(g - 2):
                    G = g - 2
                    act.wait_ge(v_ldif, per_group(G + 1, r))
                    nc.scalar.activation(lexp[:], ldif[:], ACT.Exp).then_inc(a_lexp, 1)

            act.wait_ge(s_bias, 64)
            nc.scalar.activation(tg[:], gains[:], ACT.Tanh).then_inc(s_tanh, 1)
            act.wait_ge(s_vset, 1)
            run_steps(step, act)

            def two(v, r, per=1):
                return v if r is None else r * (2 * per) + v

            def expert(e, r):
                p = e % 2
                act.wait_ge(p_eT, two(e + 1, r))
                if e >= 2:
                    act.wait_ge(p_H, two(4 * (e - 1), r, 4))
                nc.scalar.activation(xeT[p][:], S[:, p, :], ACT.Copy).then_inc(a_eT, 1)
                for f in (0, 2):
                    act.wait_ge(p_H, two(4 * e + f + 1, r, 4))
                    if e >= 2 and f == 0:
                        act.wait_ge(p_Y, two(e - 1, r))
                    nc.scalar.activation(hid[p][:, f, :], TS[:, f // 2, :], ACT.Relu, bias=b1_act[p][:, 0, f:f + 1]).then_inc(a_H, 1)
                if e < E - 1:
                    load_b1(e + 1, r)

            def load_b1(e, r):
                nc.scalar.activation(b1_act[e % 2][:], b1_all[:, bass.ds(two(e, r), 1), :], ACT.Copy)

            act.wait_ge(b12_in, 32)
            load_b1(0, None)

            expert(0, None)
            expert(1, None)
            with act.Fori(0, (E - 4) // 2) as r:
                for e in (2, 3):
                    expert(e, r)
            for e in (E - 2, E - 1):
                expert(e, None)

        @block.vector
        def _(dve):
            V = nc.vector

            def fence(i):
                return V.tensor_tensor(fence_v[:, i:i + 1], ident[:, 0:1], ident[:, 0:1], ALU.mult)

            def top(n, q, r):
                dve.wait_ge(p_S, per_batch(4 * n + q + 1, r, 4))
                if n >= 2 and q == 0:
                    dve.wait_ge(v_m, per_batch(n - 1, r))
                V.tensor_reduce(negm[n % 2][:, 4 * q:4 * q + 4], S[:, q % 2, :].rearrange("p (h k) -> p h k", h=4),
                                AX.X, ALU.max, negate=True).then_inc(v_red, 1)

            def split_copy(n, r):
                dve.wait_ge(v_red, per_batch(4 * n + 4, r, 4))
                if n >= 2:
                    dve.wait_ge(p_m, per_batch(n - 1, r))
                V.tensor_copy(mpart[n % 2][:, 0, :], negm[n % 2][:]).then_inc(v_m1, 1)

            def split_rest(n, r):
                dve.wait_ge(v_m1, per_batch(n + 1, r))
                V.tensor_tensor(mpart[n % 2][:, 1, :], negm[n % 2][:], mpart[n % 2][:, 0, :], ALU.subtract).then_inc(v_m, 1)

            def normalise(n, r):
                o = X[:, 1, :].rearrange("p (h v) -> p h v", v=HV)
                dve.wait_ge(p_back, per_batch(n + 1, r))
                if n >= 1:
                    dve.wait_ge(v_on, per_batch(n, r))
                V.reciprocal(rl[:], o[:, :, HD]).then_inc(v_rl, 1)
                dve.wait_ge(v_rl, per_batch(n + 1, r))
                if n >= 2:
                    dve.wait_ge(p_oT, per_batch(n - 1, r))
                V.tensor_tensor(on[n % 2][:].rearrange("p (h d) -> p h d", d=HD), o[:, :, 0:HD],
                                rl[:].unsqueeze(2).broadcast_to([P, HEADS, HD]), ALU.mult).then_inc(v_on, 1)

            def residual(n, r):
                dve.wait_ge(p_at, per_batch(n + 1, r))
                dve.wait_ge(g_xb, per_group(n // GB + 1, r))
                G, row1 = n // GB, rec[n // GB % 2][:, n % GB, D:2 * D]
                if n % GB == 0:
                    dve.wait_ge(sent[G % 2], per_group(64 * (G // 2) + 64, r, 32))
                    if G >= 1:
                        dve.wait_ge(x1_out, per_group(16 * G, r, 16))
                row = x_sb[:, bass.ds(per_batch(n, r), 1), :].rearrange("p o d -> p (o d)")
                V.tensor_tensor(row1, X[:, 0, 0:D], row, ALU.add).then_inc(v_x1, 1)
                dve.wait_ge(v_x1, per_batch(n + 1, r))
                V.bn_stats(st2[:, n % GB, :], row1).then_inc(v_st2, 1)

            def moments2(G, r):
                dve.wait_ge(v_st2, per_batch(GB * G + GB, r))
                fence(1)
                for k in range(GB):
                    mm = V.bn_aggr(mv2[:, k, :], st2[:, k, :])
                mm.then_inc(v_mv2, 1)

            def moments1(H, r):
                if H >= 1:
                    dve.wait_ge(v_xn, per_group(H, r))
                else:
                    dve.wait_ge(x_in[0], 16)
                if H in (1, 2):
                    dve.wait_ge(x_in[H], 16)
                fence(2)
                for k in range(GB):
                    row = x_sb[:, bass.ds(per_group(H * GB + k, r, GB), 1), :].rearrange("p o d -> p (o d)")
                    mm = V.bn_stats(st1[:, k, :], row)
                mm.then_inc(v_st1, 1)

            def gathered1(H, r):
                dve.wait_ge(v_st1, per_group(H + 1, r))
                fence(4)
                for k in range(GB):
                    mm = V.bn_aggr(mv1[:, k, :], st1[:, k, :])
                mm.then_inc(v_mv1, 1)

            def normed1(H, r, ks):
                if ks[0] == 0:
                    dve.wait_ge(g_rs1, per_group(H + 1, r))
                    if H >= 1:
                        dve.wait_ge(p_xT, per_group(H, r))
                for k in ks:
                    row = x_sb[:, bass.ds(per_group(H * GB + k, r, GB), 1), :].rearrange("p o d -> p (o d)")
                    mm = V.tensor_scalar(xn[:, k, :], row, mv1[:, k, 0:1], rs1[:, 1, k:k + 1], ALU.subtract, ALU.mult)
                return mm

            def value_rows(G, r):
                dve.wait_ge(p_v, per_group(G + 1, r))
                if G == 0:
                    dve.wait_ge(g_vals, 2)
                if G >= 2:
                    dve.wait_ge(p_O, per_batch(GB * (G - 2) + GB, r))
                V.tensor_tensor(vals[G % 2][:, :, :, 0:HD], X[:, 1, :].rearrange("p (k h d) -> p k h d", k=GB, d=HD),
                                bv[:].rearrange("p (h d) -> p h d", d=HD).unsqueeze(1).broadcast_to([P, GB, HEADS, HD]),
                                ALU.add).then_inc(v_v, 1)

            ROUTE = 4

            def route(G, r, n):
                def done(i):
                    dve.wait_ge(v_route, per_group(ROUTE * G + i, r, ROUTE))

                dve.wait_ge(v_lg, per_group(G + 1, r))
                V.tensor_reduce(lmax[:], lgs[:], AX.X, ALU.max).then_inc(v_route, 1)
                V.tensor_reduce(seen_g[:], mask[:].rearrange("p k e -> p e k"), AX.X, ALU.add)
                if is_batch(n):
                    split_copy(n, r)
                done(1)
                V.tensor_tensor(cand[:], lgs[:], lmax[:].unsqueeze(2).broadcast_to([P, GB, E]), ALU.is_lt).then_inc(v_route, 1)
                V.tensor_tensor(ldif[:], lgs[:], lmax[:].unsqueeze(2).broadcast_to([P, GB, E]), ALU.subtract).then_inc(v_ldif, 1)
                if is_batch(n):
                    split_rest(n, r)
                done(2)
                V.scalar_tensor_tensor(cand[:], cand[:], float(E), iota, ALU.mult, ALU.add).then_inc(v_route, 1)
                V.tensor_tensor(seen[:], seen[:], seen_g[:], ALU.add)
                done(3)
                V.tensor_reduce(choice[:], cand[:], AX.X, ALU.min).then_inc(v_route, 1)
                done(4)
                V.tensor_tensor(mask[:], iota, choice[:].unsqueeze(2).broadcast_to([P, GB, E]), ALU.is_equal).then_inc(v_mask, 1)

            PLACE = 2

            def logits(G, r):
                dve.wait_ge(p_lg, per_group(G + 1, r))
                if G >= 1:
                    dve.wait_ge(v_slot, per_group(G, r))
                V.tensor_copy(lgs[:].rearrange("p k e -> p (k e)"), X[:, 1, 0:GB * E]).then_inc(v_lg, 1)

            def positions(G, r):
                dve.wait_ge(p_pos, per_group(G + 1, r))
                V.tensor_tensor(at_e[:].rearrange("p k e -> p (k e)"), X[:, 1, 0:GB * E],
                                mask[:].rearrange("p k e -> p (k e)"), ALU.mult).then_inc(v_pos, 1)

            def place(G, r, n):
                def done(i):
                    dve.wait_ge(v_place, per_group(PLACE * G + i, r, PLACE))

                dve.wait_ge(v_pos, per_group(G + 1, r))
                dve.wait_ge(a_lexp, per_group(G + 1, r))
                V.tensor_reduce(loc[:], at_e[:], AX.X, ALU.add)
                V.tensor_reduce(lsum[:], lexp[:], AX.X, ALU.add).then_inc(v_place, 1)
                V.tensor_copy(rec[G % 2][:, :, 2 * D + 1], token_code[:, bass.ds(per_group(G * GB, r, GB), GB)])
                if is_batch(n):
                    split_copy(n, r)
                done(1)
                V.tensor_scalar(over[:], loc[:], float(CAP), float(NONE), ALU.is_ge, ALU.mult)
                V.scalar_tensor_tensor(base[:], choice[:], float(CAP), loc[:], ALU.mult, ALU.add).then_inc(v_place, 1)
                V.reciprocal(rec[G % 2][:, :, 2 * D], lsum[:])
                if is_batch(n):
                    split_rest(n, r)
                done(2)
                V.tensor_tensor(slot[G % 2][:], base[:], over[:], ALU.add).then_inc(v_slot, 1)

            def step(c, r):
                j, g = c % GB, c // GB
                if is_batch(c):
                    top(c, 0, r)
                if j == 1 and is_group(g):
                    value_rows(g, r)
                if is_batch(c - 5):
                    residual(c - 5, r)
                if is_batch(c):
                    top(c, 1, r)
                if j == 2 and is_group(g + 2):
                    normed1(g + 2, r, (2, 3)).then_inc(v_xn, 1)
                if is_batch(c - 4):
                    normalise(c - 4, r)
                if j == 0 and is_group(g - 2):
                    moments2(g - 2, r)
                if j == 1 and is_group(g + 2):
                    gathered1(g + 2, r)
                if is_batch(c):
                    top(c, 2, r)
                if j == 2 and is_group(g - 2):
                    logits(g - 2, r)
                if j == 3 and is_group(g - 2):
                    positions(g - 2, r)
                if is_batch(c):
                    top(c, 3, r)
                if j == 2 and is_group(g - 2):
                    route(g - 2, r, c)
                elif j == 3 and is_group(g - 2):
                    place(g - 2, r, c)
                elif is_batch(c):
                    split_copy(c, r)
                    split_rest(c, r)
                if j == 2 and g + 2 == 0:
                    split(dve, V, 1, 0, None)
                if j == 0 and is_group(g + 2):
                    moments1(g + 2, r)
                if j == 1 and is_group(g + 2):
                    normed1(g + 2, r, (0, 1))

            dve.wait_ge(s_cst, 16)
            V.tensor_copy(ident_b[:], ident)
            V.tensor_copy(before_b[:], cst[:, P:2 * P])
            V.memset(ones_b[:], 1.0)
            V.memset(mask[:], 0.0)
            V.memset(seen[:], 0.0)
            V.memset(ones_row[:], 1.0).then_inc(v_ones, 1)
            dve.wait_ge(s_wqkv, 16)
            dve.wait_ge(s_bias, 64)
            V.tensor_scalar(bq_s[:], bqk[:, 0:1], SCALE, None, ALU.mult)
            V.tensor_copy(wq_dh[:].rearrange("p (d h) -> p d h", h=HEADS), wqkv[:, 0:D].rearrange("p (h d) -> p d h", d=HD))
            V.tensor_copy(wk_dh[:].rearrange("p (d h) -> p d h", h=HEADS),
                          wqkv[:, D:2 * D].rearrange("p (h d) -> p d h", d=HD)).then_inc(s_vset, 1)

            for c in range(FIRST, LOOP0):
                if c == -4:
                    dve.wait_ge(s_late, 64)
                    dve.wait_ge(s_tanh, 1)
                    V.tensor_scalar(wout_g[:], wout[:], tg[:, 0:1], None, ALU.mult)
                    V.tensor_scalar(bout_g[:], bout[:], tg[:, 0:1], None, ALU.mult).then_inc(s_vset, 1)
                step(c, None)
            with dve.Fori(0, (LOOP1 - LOOP0) // BODY) as r:
                for c in range(LOOP0, LOOP0 + BODY):
                    step(c, r)
            for c in range(LOOP1, LAST + 1):
                step(c, None)

            def two(v, r, per=1):
                return v if r is None else r * (2 * per) + v

            def relus(e, r):
                p = e % 2
                for f in (1, 3):
                    dve.wait_ge(p_H, two(4 * e + f + 1, r, 4))
                    if e >= 2 and f == 1:
                        dve.wait_ge(p_Y, two(e - 1, r))
                    if f == 1 and e < E - 1:
                        if e >= 1:
                            dve.wait_ge(v_H, two(2 * e, r, 2))
                        load_b1(e + 1, r)
                    V.tensor_scalar(hid[p][:, f, :], O[:, f // 2, :], b1_dve[p][:, 0, f:f + 1], 0.0, ALU.add, ALU.max).then_inc(v_H, 1)

            def load_b1(e, r):
                return V.tensor_copy(b1_dve[e % 2][:], b1_all[:, bass.ds(two(e, r), 1), :])

            def finish(e, r):
                p = e % 2
                dve.wait_ge(xr_in[p], two(16 * (e // 2) + 16, r, 8))
                if e >= 2:
                    dve.wait_ge(fin_out[p], two(64 * (e // 2), r, 32))
                V.tensor_scalar(gate2[p][:], xr[p][:, :, D], tg[:, 1:2], None, ALU.mult).then_inc(v_gate2, 1)
                V.tensor_scalar(tok[p][:], xr[p][:, :, D + 1], -1.0, float(NONE), ALU.mult, ALU.add).then_inc(v_tok, 1)
                dve.wait_ge(p_Y, two(e + 1, r))
                if e >= 1:
                    dve.wait_ge(v_fin, two(e, r))
                V.tensor_tensor(yb[:].rearrange("p (t n) -> p t n", n=D), X[:, p, :].rearrange("p (t n) -> p t n", n=D),
                                b2_all[:, bass.ds(two(e, r), 1), :].broadcast_to([P, ET, D]), ALU.add).then_inc(v_yb, 1)
                dve.wait_ge(v_yb, two(e + 1, r))
                for t in range(ET):
                    mm = V.scalar_tensor_tensor(fin[p][:, t, :], yb[:, t * D:(t + 1) * D], gate2[p][:, t:t + 1],
                                                xr[p][:, t, 0:D], ALU.mult, ALU.add)
                mm.then_inc(v_fin, 1)

            dve.wait_ge(b12_in, 32)
            load_b1(0, None).then_inc(v_b1, 1)
            dve.wait_ge(v_b1, 1)
            relus(0, None)
            relus(1, None)
            finish(0, None)
            relus(2, None)
            finish(1, None)
            with dve.Fori(0, (E - 4) // 2) as r:
                for e in (3, 4):
                    relus(e, r)
                    finish(e - 1, r)
            relus(E - 1, None)
            finish(E - 2, None)
            finish(E - 1, None)

        @block.gpsimd
        def _(pool):
            G_ = nc.gpsimd

            def fence():
                return G_.tensor_tensor(fence_p[:], pool_c[:, 0, 0:1], pool_c[:, 0, 0:1], ALU.add).then_inc(g_fence, 1)

            def root(H, r, mv, rs, ready, e):
                pool.wait_ge(ready, per_group(H + 1, r))
                G_.tensor_tensor(rs[:, 0, :], mv[:, :, 1], pool_c[:, 0, :], ALU.add).then_inc(e, 1)
                pool.wait_ge(e, per_group(H + 1, r))
                return G_.tensor_tensor(rs[:, 1, :], rs[:, 0, :], pool_c[:, 1, :], ALU.pow)

            def norm2(G, r):
                to, spread = rec[G % 2][:, :, 0:D], [P, GB, D]
                root(G, r, mv2, rs2, v_mv2, g_e2)
                G_.tensor_tensor(to, rec[G % 2][:, :, D:2 * D], mv2[:, :, 0:1].broadcast_to(spread), ALU.subtract).then_inc(g_rs2, 1)
                pool.wait_ge(g_rs2, per_group(G + 1, r))
                G_.tensor_tensor(to, to, rs2[:, 1, :].unsqueeze(2).broadcast_to(spread), ALU.mult).then_inc(g_xn2, 1)

            def scatter(G, r):
                p = G % 2
                if G == 0:
                    for q in sent:
                        pool.wait_ge(q, 64)
                pool.wait_ge(v_slot, per_group(G + 1, r))
                if G == NG - 1:
                    pool.wait_ge(g_fence, NG - 1)
                fence()
                for k in range(GB):
                    G_.indirect_dma_start(rec_dram, bass.IndirectOffsetOnAxis(slot[p][:, k:k + 1], 0), rec[p][:, k, :], None,
                                          bounds_check=T - 1, oob_is_err=False).then_inc(sent[p], 16)

            def step(c, r):
                j, g = c % GB, c // GB
                if j == 0 and is_group(g - 2):
                    norm2(g - 2, r)
                if j == 0 and g - 3 == NG - 2:
                    scatter(NG - 2, None)
                if j == 1 and is_group(g + 2):
                    root(g + 2, r, mv1, rs1, v_mv1, g_e1).then_inc(g_rs1, 1)
                for i in {-7: (0, 1), 0: (2,), 1: (3,), 2: (4,), 3: (5,), 4: (6,), 5: (7,)}.get(c, ()):
                    zero_records(i)
                if j == 1 and is_group(g + 1):
                    split(pool, G_, 0, g + 1, r)
                if j == 2 and is_group(g + 1):
                    H = g + 1
                    pool.wait_ge(v_xn, per_group(H + 1, r))
                    if H <= 0:
                        pool.wait_ge(s_vset, 2)
                    rows = x_sb[:, bass.ds(per_group(H * GB, r, GB), GB), :]
                    G_.tensor_tensor(rows, rows, bout_g[:].unsqueeze(1).broadcast_to([P, GB, D]), ALU.add).then_inc(g_xb, 1)
                if j == 3 and is_group(g + 2) and g + 2 != 0:
                    split(pool, G_, 1, g + 2, r)
                if j == 3 and is_group(g - 2) and g - 2 != NG - 2:
                    scatter(g - 2, r)

            ZEROED = 8

            def zero_records(i):
                pool.dma_start(rec_dram[i * (T // ZEROED):(i + 1) * (T // ZEROED), :].rearrange("(p a) c -> p a c", p=P),
                               zeros[:].unsqueeze(1).broadcast_to([P, T // P // ZEROED, REC])).then_inc(sent[i % 2], 16)

            G_.memset(pool_c[:, 0, :], EPS)
            G_.memset(pool_c[:, 1, :], -0.5).then_inc(s_pset, 1)
            G_.memset(zeros[:], 0.0).then_inc(s_zero, 1)
            pool.wait_ge(s_zero, 1)
            for i in range(2):
                G_.memset(vals[i][:, :, :, HD:HV], 0.0).then_inc(g_zero, 1)
            pool.wait_ge(g_zero, 2)
            for i in range(2):
                G_.memset(vals[i][:, :, :, HD:HD + 1], 1.0).then_inc(g_vals, 1)
            pool.wait_ge(s_pset, 1)
            run_steps(step, pool)

            def rows_out(e, r):
                p = e % 2
                pool.wait_ge(v_fin, e + 1 if r is None else r * 2 + (e + 1))
                pool.wait_ge(v_tok, e + 1 if r is None else r * 2 + (e + 1))
                pool.wait_ge(g_fence, r * 2 + (NG + e))
                fence()
                for t in range(ET):
                    G_.indirect_dma_start(out_rows, bass.IndirectOffsetOnAxis(tok[p][:, t:t + 1], 0), fin[p][:, t, :], None,
                                          bounds_check=T - 1, oob_is_err=False).then_inc(fin_out[p], 16)

            pool.wait_ge(x1_out, 16 * NG)
            with pool.Fori(0, E // 2) as r:
                for e in (0, 1):
                    rows_out(e, r)


_INS = ['x', 'ctx_1024', 'g_xattn', 'g_ffn', 'L0_xattn_W_qkv', 'L0_xattn_b_qkv', 'L0_xattn_W_out', 'L0_xattn_b_out',
        'L0_ffn_Wg', 'L0_ffn_W1', 'L0_ffn_b1', 'L0_ffn_W2', 'L0_ffn_b2']


def kernel(**inputs):
    import numpy as _np
    import concourse.bacc as _bacc
    from concourse import mybir as _mybir
    from concourse.bass_utils import run_bass_kernel_spmd as _run

    nc = _bacc.Bacc("TRN2", target_bir_lowering=False, num_devices=1)
    arrays, args = {}, []
    for name in _INS:
        a = _np.ascontiguousarray(inputs[name])
        arrays[f"in_{name}_dram"] = a
        args.append(nc.dram_tensor(f"in_{name}_dram", a.shape, _mybir.dt.from_np(a.dtype), kind="ExternalInput").ap())
    n_b, n_e, n_k = inputs['x'].shape[0], inputs['L0_ffn_Wg'].shape[1], GB
    tokens = _np.arange(n_b * P, dtype=_np.float32).reshape(n_b, P).T
    consts = _np.concatenate([_np.eye(P), _np.triu(_np.ones((P, P)), 1),
                              _np.tile(_np.arange(n_e), (P, n_k)), 2 * n_b * P - tokens], axis=1).astype(_np.float32)
    arrays["in_consts_dram"] = consts
    args.append(nc.dram_tensor("in_consts_dram", consts.shape, _mybir.dt.float32, kind="ExternalInput").ap())
    shape = tuple(inputs['x'].shape)
    args.append(nc.dram_tensor("out_0_dram", shape, _mybir.dt.float32, kind="ExternalOutput").ap())
    flamingo_kernel(nc, *args)
    r = _run(nc, [arrays], core_ids=[0])
    return r.results[0]["out_0_dram"]
```
